# Optimizing a Trainium2 kernel written in Bass

```python
import numpy as np
import jax
import jax.numpy as jnp

def _softmax(x, axis=-1):
    return jax.nn.softmax(x, axis=axis)

def _gelu(x):
    return jax.nn.gelu(x, approximate=True)

def _silu(x):
    return jax.nn.silu(x)

def _sigmoid(x):
    return jax.nn.sigmoid(x)

def _layernorm(x, axis=-1, eps=1e-05):
    m = jnp.mean(x, axis=axis, keepdims=True)
    v = jnp.var(x, axis=axis, keepdims=True)
    return (x - m) / jnp.sqrt(v + eps)

def _scatter_add(tgt, idx, src, axis=0):
    return tgt.at[idx].add(src)

def _segment_sum(src, seg, n):
    return jax.ops.segment_sum(src, seg, n)
kernel_name = 'mk_gnn_preln_d2_gnn_r32_db0362'

def setup_inputs(seed: int=0):
    np.random.seed(seed)
    _w = jnp.asarray

    def _rec_inputs():
        import jax
        import jax.numpy as jnp
        _gk = jax.random.key(seed)
        x = -0.0003929 + 0.9999 * jax.random.normal(jax.random.fold_in(_gk, 1), (512, 1024), jnp.float32)
        src = jax.random.randint(jax.random.fold_in(_gk, 2), (8192,), 0, 512, jnp.int32)
        dst = jax.random.randint(jax.random.fold_in(_gk, 3), (8192,), 0, 512, jnp.int32)
        _o = jnp.argsort(dst, stable=True)
        src = src[_o]
        dst = dst[_o]
        return (x, src, dst)
    x, src, dst = _rec_inputs()

    def _L0_gnn_setup():
        import jax, jax.numpy as jnp
        import numpy as np
        NH, NO = (128, 384)
        N = NH + NO
        E_HH, E_OO, E_HO = (256, 1280, 512)
        E = E_HH + E_OO + E_HO
        D = 1024
        key = jax.random.key(seed)
        ks = jax.random.split(key, 12)
        w = lambda k, s: jax.random.normal(k, s, jnp.float32) * 0.02
        return {'n_f': jax.random.normal(ks[0], (N, D), jnp.float32), 'W_hh': w(ks[1], (2 * D, D)), 'b_hh': jnp.zeros((D,), jnp.float32), 'W_oo': w(ks[2], (2 * D, D)), 'b_oo': jnp.zeros((D,), jnp.float32), 'W_ho': w(ks[3], (2 * D, D)), 'b_ho': jnp.zeros((D,), jnp.float32), 'W_a': w(ks[4], (D, 1)), 'b_a': jnp.zeros((1,), jnp.float32), 'W_hn': w(ks[5], (2 * D, D)), 'b_hn': jnp.zeros((D,), jnp.float32), 'W_on': w(ks[6], (2 * D, D)), 'b_on': jnp.zeros((D,), jnp.float32), 'edge_src': jax.random.randint(ks[7], (E,), 0, N, jnp.int32), 'edge_dst': jax.random.randint(ks[8], (E,), 0, N, jnp.int32)}
    _L0_gnn_all = _L0_gnn_setup()
    _L0_gnn_in = {k: v for k, v in _L0_gnn_all.items() if k in ('W_hh', 'b_hh', 'W_oo', 'b_oo', 'W_ho', 'b_ho', 'W_a', 'b_a', 'W_hn', 'b_hn', 'W_on', 'b_on')}
    del _L0_gnn_all

    def _L1_gnn_setup():
        import jax, jax.numpy as jnp
        import numpy as np
        N = 625
        E = 10000
        D_IN = 1024
        D_OUT = 1024
        key = jax.random.key(seed)
        k1, k2, k3, k4 = jax.random.split(key, 4)
        x = jax.random.normal(k1, (N, D_IN), dtype=jnp.float32)
        edge_index = jax.random.randint(k2, (2, E), 0, N, dtype=jnp.int64)
        W = jax.random.normal(k3, (D_OUT, D_IN), dtype=jnp.float32) * (1.0 / np.sqrt(D_IN))
        b = jax.random.normal(k4, (D_OUT,), dtype=jnp.float32) * 0.01
        return {'x': x, 'edge_index': edge_index, 'W': W, 'b': b}
    _L1_gnn_all = _L1_gnn_setup()
    _L1_gnn_in = {k: v for k, v in _L1_gnn_all.items() if k in ('W', 'b')}
    del _L1_gnn_all
    return {'x': x, 'src': src, 'dst': dst, 'L0_gnn_W_hh': _L0_gnn_in['W_hh'], 'L0_gnn_b_hh': _L0_gnn_in['b_hh'], 'L0_gnn_W_oo': _L0_gnn_in['W_oo'], 'L0_gnn_b_oo': _L0_gnn_in['b_oo'], 'L0_gnn_W_ho': _L0_gnn_in['W_ho'], 'L0_gnn_b_ho': _L0_gnn_in['b_ho'], 'L0_gnn_W_a': _L0_gnn_in['W_a'], 'L0_gnn_b_a': _L0_gnn_in['b_a'], 'L0_gnn_W_hn': _L0_gnn_in['W_hn'], 'L0_gnn_b_hn': _L0_gnn_in['b_hn'], 'L0_gnn_W_on': _L0_gnn_in['W_on'], 'L0_gnn_b_on': _L0_gnn_in['b_on'], 'L1_gnn_W': _L1_gnn_in['W'], 'L1_gnn_b': _L1_gnn_in['b']}

def reference(x, src, dst, L0_gnn_W_hh, L0_gnn_b_hh, L0_gnn_W_oo, L0_gnn_b_oo, L0_gnn_W_ho, L0_gnn_b_ho, L0_gnn_W_a, L0_gnn_b_a, L0_gnn_W_hn, L0_gnn_b_hn, L0_gnn_W_on, L0_gnn_b_on, L1_gnn_W, L1_gnn_b):
    import jax
    import jax.numpy as jnp

    def _L0_gnn_ref(n_f, W_hh, b_hh, W_oo, b_oo, W_ho, b_ho, W_a, b_a, W_hn, b_hn, W_on, b_on, edge_src, edge_dst):
        import jax, jax.numpy as jnp
        import numpy as np
        NH, NO = (128, 384)
        N = NH + NO
        E_HH, E_OO, E_HO = (256, 1280, 512)
        E = E_HH + E_OO + E_HO
        D = 1024
        feat = jnp.concatenate([n_f[edge_src], n_f[edge_dst]], axis=1)
        e_hh = jax.nn.relu(feat[:E_HH] @ W_hh + b_hh)
        e_oo = jax.nn.relu(feat[E_HH:E_HH + E_OO] @ W_oo + b_oo)
        e_ho = jax.nn.relu(feat[E_HH + E_OO:] @ W_ho + b_ho)
        e_f = jnp.concatenate([e_hh, e_oo, e_ho], axis=0)
        logit = (e_f @ W_a + b_a)[:, 0]
        m = jax.lax.stop_gradient(jax.ops.segment_max(logit, edge_dst, num_segments=N))
        ex = jnp.exp(logit - m[edge_dst])
        den = jax.ops.segment_sum(ex, edge_dst, num_segments=N)
        alpha = ex / den[edge_dst]
        z_f = jax.ops.segment_sum(alpha[:, None] * n_f[edge_src], edge_dst, num_segments=N)
        nf2 = jnp.concatenate([n_f, z_f], axis=1)
        h_new = jax.nn.relu(nf2[:NH] @ W_hn + b_hn)
        o_new = jax.nn.relu(nf2[NH:] @ W_on + b_on)
        return jnp.concatenate([h_new, o_new], axis=0)

    def _L1_gnn_ref(x, edge_index, W, b):
        import jax, jax.numpy as jnp
        import numpy as np
        N = 625
        E = 10000
        D_IN = 1024
        D_OUT = 1024
        num_nodes = x.shape[0]
        self_idx = jnp.arange(num_nodes, dtype=edge_index.dtype)
        ei = jnp.concatenate([edge_index, jnp.stack([self_idx, self_idx], axis=0)], axis=1)
        row, col = (ei[0], ei[1])
        h = jnp.einsum('nd,od->no', x, W) + b
        deg = jnp.zeros((num_nodes,), dtype=h.dtype).at[row].add(1.0)
        deg_inv_sqrt = deg ** (-0.5)
        norm = deg_inv_sqrt[row] * deg_inv_sqrt[col]
        msg = norm[:, None] * h[col]
        out = jax.ops.segment_sum(msg, row, num_segments=num_nodes)
        return out
    edge_index = jnp.stack([src, dst])
    h = jnp.maximum(_layernorm(x, axis=-1), 0.0)
    x = x + _L0_gnn_ref(h, L0_gnn_W_hh, L0_gnn_b_hh, L0_gnn_W_oo, L0_gnn_b_oo, L0_gnn_W_ho, L0_gnn_b_ho, L0_gnn_W_a, L0_gnn_b_a, L0_gnn_W_hn, L0_gnn_b_hn, L0_gnn_W_on, L0_gnn_b_on, src, dst)
    h = jnp.maximum(_layernorm(x, axis=-1), 0.0)
    x = x + _L1_gnn_ref(h, edge_index, L1_gnn_W, L1_gnn_b)
    return x

_drawn_inputs = setup_inputs


def setup_inputs(seed=0):
    import zlib

    import numpy as np

    out = dict(_drawn_inputs(seed))
    spreads = {'L0_gnn_b_hh': (0.0, 2.0),
     'L0_gnn_b_oo': (0.0, 2.0),
     'L0_gnn_b_ho': (0.0, 0.8),
     'L0_gnn_b_hn': (0.0, 0.1),
     'L0_gnn_b_on': (0.0, 0.1)}
    factors = {'L0_gnn_W_hh': 8.0,
     'L0_gnn_W_oo': 8.0,
     'L0_gnn_W_ho': 6.871,
     'L0_gnn_W_a': 6.513,
     'L1_gnn_b': 6.819}
    for name, (base, spread) in spreads.items():
        noise = np.random.default_rng([zlib.crc32(name.encode()), seed]).standard_normal(out[name].shape)
        drawn = base * np.exp(spread * noise) if base else spread * noise
        out[name] = jnp.asarray(drawn.astype(out[name].dtype))
    for name, factor in factors.items():
        out[name] = (out[name] * factor).astype(out[name].dtype)
    return out
```

```python
from contextlib import ExitStack

import concourse.bass as bass
from concourse import mybir

P = 128
FB = 512
KB = 1024
ALU = mybir.AluOpType
ACT = mybir.ActivationFunctionType
AX = mybir.AxisListType
F32 = mybir.dt.float32
F32R = mybir.dt.float32r
U16 = mybir.dt.uint16
I32 = mybir.dt.int32
U32 = mybir.dt.uint32

E_HH, E_OO = 256, 1280
NH = 128
EPS = 1e-5
BIG = 1e30


def gnn_kernel(nc, x, src, dst, W_hh, b_hh, W_oo, b_oo, W_ho, b_ho, W_a, b_a,
               W_hn, b_hn, W_on, b_on, W1, b1, out):
    N, D = x.shape
    E = src.shape[0]
    NM = N // P
    KT = D // P
    NN = D // FB
    ET = E // P
    T_HH, T_OO = E_HH // P, E_OO // P
    T_HO = ET - T_HH - T_OO
    EARLY = T_HH + T_OO
    assert NM == 4 and KT == 8 and NN == 2 and N == FB and NH == P

    with ExitStack() as ctx:
        def sem(name):
            return ctx.enter_context(nc.semaphore(name))

        BASE = 16512
        assert BASE >= nc.sbuf_base
        at = {}

        def sb(name, shape, dt, size=None, over=None, shift=0):
            width = mybir.dt.size(dt)
            for n in shape[1:]:
                width *= n
            if over is None:
                off = at.get("end", BASE)
                at["end"] = off + -(-(size or width) // 32) * 32
            else:
                off = at[over] + shift
            at[name] = off
            return nc.alloc_sbuf_tensor_at(name, shape, dt, offset=off)

        actT_h = sb("actT_h", [P, KT, N], F32R)
        actT_l = sb("actT_l", [P, KT, N], F32R)
        hrow = sb("hrow", [P, NM, D], F32)
        ring_h = sb("ring_h", [P, KT, FB], F32R)
        ring_l = sb("ring_l", [P, KT, FB], F32R)
        RAW = 4
        raw = sb("raw", [P, RAW, FB], F32)
        GB = 4
        gath_a = sb("gath_a", [P, GB, D], F32)
        gath_b = sb("gath_b", [P, GB, D], F32)
        logit_d = sb("logit_d", [P, 3, NM, N], F32)
        count_d = sb("count_d", [P, 3, NM, N], U16)
        onehot = sb("onehot", [P, 2, 4, N], F32R)
        stage = sb("stage", [P, 4, FB], F32)
        bias3 = sb("bias3", [P, 3, D], F32)
        wa_b = sb("wa_b", [P, D], F32)
        iota_f = sb("iota_f", [P, N], F32)
        ident = sb("ident", [P, P], F32)
        zeros_r = sb("zeros_r", [P, N], F32R)
        rows_i = sb("rows_i", [ET, 2, P], I32)
        rows_f = sb("rows_f", [ET, 2, P], F32)
        node_f = sb("node_f", [P, ET, 2], F32)
        tabl_f = sb("tabl_f", [P, ET, 2], F32)
        tabl_i = sb("tabl_i", [P, ET, 2], U32)
        tabl_s = sb("tabl_s", [P, GB, 2], U32)
        lg = sb("lg", [P, ET], F32)
        lgb = sb("lgb", [P, ET], F32)
        lgh = sb("lgh", [P, ET], F32R)
        lgl = sb("lgl", [P, ET], F32)
        ba = sb("ba", [P, 1], F32)
        stats = sb("stats", [P, NM, 2, 6], F32)
        mv = sb("mv", [P, NM, 2], F32)
        rstd = sb("rstd", [P, NM], F32)
        mx3 = sb("mx3", [P, 3, NM], F32)
        mx = sb("mx", [P, NM], F32)
        nmx = sb("nmx", [P, NM], F32)
        den = sb("den", [P, NM], F32)
        rden = sb("rden", [P, NM], F32)
        rowid = sb("rowid", [P, NM], F32)
        ones = sb("ones", [P, 1], F32)
        var_e = sb("var_e", [P, NM], F32)
        rs_in = sb("rs_in", [P, NM], F32)
        rs_root = sb("rs_root", [P, NM], F32)
        rs_t = sb("rs_t", [P, NM], F32)
        dinv = sb("dinv", [P, NM], F32)
        wrow = sb("wrow", [P, NM], F32)
        assert at["end"] <= nc.sbuf_usable_end, at["end"] - nc.sbuf_usable_end

        w1row = sb("w1row", [P, KT, D], F32, over="gath_b")
        w1t_s = sb("w1t_s", [P, 4, FB], F32, over="onehot")
        hrow_h = sb("hrow_h", [P, NM, D], F32R, over="gath_a")
        hrow_l = sb("hrow_l", [P, NM, D], F32R, over="gath_b")
        topsum = sb("topsum", [P, NM, D], F32, over="onehot")
        attT_h = sb("attT_h", [P, NM, N], F32R, over="logit_d", shift=4 * NM * N)
        attT_l = sb("attT_l", [P, NM, N], F32R, over="logit_d", shift=8 * NM * N)
        adj = sb("adj", [P, NM, N], F32, over="stage")
        adj_h = sb("adj_h", [P, NM, N], F32R, over="logit_d")
        adj_l = sb("adj_l", [P, NM, N], F32R, over="count_d")

        ps = ctx.enter_context(nc.psum_tensor("ps", [P, 8, FB], F32))
        tab_a = nc.dram_tensor("tab_a", [3 * N, D], F32).ap()
        tab_b = nc.dram_tensor("tab_b", [3 * N, D], F32).ap()
        w1t = nc.dram_tensor("w1t", [D, D], F32).ap()

        s_x = [sem(f"x_loaded{m}") for m in range(NM)]
        s_idx = sem("edges_loaded")
        s_const = sem("consts_loaded")
        s_bias = sem("bias_loaded")
        s_bias2 = sem("bias2_loaded")
        s_w1row = sem("w1_loaded")
        s_w1t = sem("w1t_banks")
        s_w1e = sem("w1t_copied")
        s_w1st = [sem(f"w1t_stored{i}") for i in range(4)]
        s_raw = [sem(f"raw_loaded{i}") for i in range(RAW)]
        s_high = sem("w_high_ready")
        s_low = sem("w_low_ready")
        s_slot = sem("w_slots_free")
        s_afree = sem("a_banks_free")
        s_bfree = sem("b_banks_free")
        s_ast = [sem(f"a_stored{i}") for i in range(2)]
        s_bst = [sem(f"b_stored{i}") for i in range(2)]
        s_esum = sem("edge_sums")
        s_pool = sem("pool_chain")
        s_gconst = sem("consts_made")
        s_v = sem("vector_chain")
        s_rsin = sem("rsqrt_input")
        s_root = sem("square_roots")
        s_h = sem("h_rows")
        s_norm = sem("h_normed")
        s_tp = sem("transposed_banks")
        s_th = sem("transposed_high")
        s_tl = sem("transposed_low")
        s_idxT = sem("edges_transposed")
        s_idxok = sem("edges_ready")
        s_g = [sem(f"gathered{i}") for i in range(GB)]
        s_edge = sem("gather_slots_free")
        s_stg = sem("index_staged")
        s_seen = sem("index_seen")
        s_oh = sem("onehots_ready")
        s_ohu = sem("onehot_slots_free")
        s_kind = sem("kind_counted")
        s_kfree = sem("kind_banks_free")
        s_mx = sem("row_max_ready")
        s_exp = sem("exp_done")
        s_att = sem("attention_ready")
        s_top = sem("top_banks_free")
        s_hr_h = sem("rows_high")
        s_hr_l = sem("rows_low")
        s_xr = [sem(f"residual_loaded{m}") for m in range(NM)]
        s_bsum = sem("update_summed")
        s_brelu = sem("update_relu")
        s_x1 = sem("x1_ready")
        s_adj = sem("adj_ready")
        s_adjs = sem("adj_split")
        s_deg = sem("deg_banks")
        s_dinv = sem("dinv_ready")
        s_out = sem("out_rows")
        s_outst = [sem(f"out_stored{i}") for i in range(2 * NM)]


        def passes(hi, lo, mh, ml):
            return ((hi, mh), (hi, ml), (lo, mh))

        block = ctx.enter_context(nc.Block())

        KINDS = ((W_ho, b_ho), (W_oo, b_oo), (W_hh, b_hh))
        CH_EDGE = 3 * 2 * NN
        NODE = [[(w, r, n, ms) for w, ms in ((W_hn, (0,)), (W_on, (1, 2, 3))) for n in range(NN)] for r in (0, D)]
        LAST = [(w1t, 0, n, (0, 1, 2, 3)) for n in range(NN)]

        @block.sync
        def _(sp):
            for m in range(NM):
                sp.dma_start(gath_a[:, m, :], x[m * P:(m + 1) * P, :]).then_inc(s_x[m], 16)
            sp.dma_start(w1row[:, :, :], W1.rearrange("(o p) i -> p o i", p=P)).then_inc(s_w1row, 16)

            def load(w, row, n, q, k):
                sp.wait_ge(s_low, q * KT + k + 1)
                sp.dma_start(raw[:, k % RAW, :], w[bass.ds(row + k * P, P), n * FB:(n + 1) * FB]).then_inc(s_raw[k % RAW], 16)

            for t, (w, _) in enumerate(KINDS):
                with sp.Fori(0, 2) as half:
                    for n in range(NN):
                        for k in range(KT):
                            load(w, half * D, n, (half * NN + n) + t * 2 * NN, k)
            q = CH_EDGE
            for w, row, n, _ in NODE[0] + NODE[1]:
                for k in range(KT):
                    load(w, row, n, q, k)
                q += 1
            for i in range(4):
                sp.wait_ge(s_w1st[i], 16 * 4)
            for w, row, n, _ in LAST:
                for k in range(KT):
                    load(w, row, n, q, k)
                q += 1
            for n in range(NN):
                for m in range(NM):
                    i = n * NM + m
                    sp.wait_ge(s_out, i + 1)
                    sp.dma_start(out[m * P:(m + 1) * P, n * FB:(n + 1) * FB], topsum[:, m, n * FB:(n + 1) * FB]).then_inc(s_outst[i], 16)
            for i in range(2 * NM):
                sp.wait_ge(s_outst[i], 16)

        @block.gpsimd
        def _(pool):
            for j, e in enumerate((src, dst)):
                rows = e.rearrange("(t p) -> t p", p=P)
                pool.dma_start(rows_i[0:T_HO, j, :], rows[EARLY:ET, :]).then_inc(s_idx, 16)
                pool.dma_start(rows_i[T_HO:ET, j, :], rows[0:EARLY, :]).then_inc(s_idx, 16)
            pool.dma_start(wa_b[:, :], W_a.rearrange("d a -> a d").partition_broadcast(P)).then_inc(s_const, 16)
            pool.dma_start(ba[:, :], b_a.rearrange("(a d) -> a d", a=1).partition_broadcast(P)).then_inc(s_const, 16)
            for t, (_, b) in enumerate(KINDS):
                pool.dma_start(bias3[:, t, :], b.rearrange("(a d) -> a d", a=1).partition_broadcast(P)).then_inc(s_bias, 16)
            nc.gpsimd.memset(ident[:, :], 0.0).then_inc(s_pool, 1)
            pool.wait_ge(s_pool, 1)
            nc.gpsimd.affine_select(out=ident[:, :], in_=ident[:, :], compare_op=ALU.not_equal, fill=1.0,
                                    base=0, pattern=[[-1, P]], channel_multiplier=1).then_inc(s_gconst, 1)
            nc.gpsimd.iota(iota_f[:, :], [[1, N]], base=0, channel_multiplier=0,
                           allow_small_or_imprecise_dtypes=True).then_inc(s_gconst, 1)
            nc.gpsimd.iota(rowid[:, :], [[P, NM]], base=0, channel_multiplier=1,
                           allow_small_or_imprecise_dtypes=True).then_inc(s_gconst, 1)
            nc.gpsimd.memset(ones[:, :], 1.0).then_inc(s_gconst, 1)
            nc.gpsimd.memset(zeros_r[:, :].bitcast(F32), 0.0).then_inc(s_gconst, 1)

            pool.wait_ge(s_idxok, 1)

            def gather(q, s, rows):
                pool.wait_ge(s_edge, q + 1)
                nc.gpsimd.tensor_copy(tabl_s[:, s, :], tabl_i[:, bass.ds(q, 1), :].rearrange("p a b -> p (a b)")).then_inc(s_stg, 1)
                pool.wait_ge(s_stg, q + 1)
                pool.sem_inc(s_seen, 1)
                for j, (buf, tab) in enumerate(((gath_a, tab_a), (gath_b, tab_b))):
                    pool.indirect_dma_start(out=buf[:, s, :], out_offset=None, in_=tab[0:rows, :],
                                            in_offset=bass.IndirectOffsetOnAxis(ap=tabl_s[:, s, j:j + 1], axis=0)
                                            ).then_inc(s_g[s], 16)

            for i in range(2):
                pool.wait_ge(s_ast[i], 16 * 4)
                pool.wait_ge(s_bst[i], 16 * 4)
            with pool.Fori(0, T_HO // GB) as i:
                for s in range(GB):
                    gather(i * GB + s, s, N)
            for i in range(2):
                pool.wait_ge(s_ast[i], 16 * 12)
                pool.wait_ge(s_bst[i], 16 * 12)
            with pool.Fori(T_HO // GB, ET // GB) as i:
                for s in range(GB):
                    gather(i * GB + s, s, 3 * N)
            pool.wait_ge(s_bfree, 8 + 3 * 8)
            for t, b in enumerate((b_hn, b_on, b1)):
                pool.dma_start(bias3[:, t, :], b.rearrange("(a d) -> a d", a=1).partition_broadcast(P)).then_inc(s_bias2, 16)
            pool.wait_ge(s_hr_l, NM)
            for m in range(NM):
                pool.dma_start(hrow[:, m, :], x[m * P:(m + 1) * P, :]).then_inc(s_xr[m], 16)

        UPD = [(0, 0), (0, 1), (1, 0), (2, 0), (3, 0), (1, 1), (2, 1), (3, 1)]
        UPD_CHUNK = [0, 1, 2, 2, 2, 3, 3, 3]

        def chunk_done(eng, q):
            eng.wait_ge(s_slot, KT + q * KT + KT)

        @block.scalar
        def _(act):
            for b in range(NN * KT):
                n, k = b // KT, b % KT
                act.wait_ge(s_w1t, b + 1)
                if b >= 4:
                    act.wait_ge(s_w1st[b % 4], 16 * (b // 4))
                nc.scalar.copy(w1t_s[:, b % 4, :], ps[:, b % 8, :]).then_inc(s_w1e, 1)
                act.wait_ge(s_w1e, b + 1)
                act.dma_start(w1t[k * P:(k + 1) * P, n * FB:(n + 1) * FB], w1t_s[:, b % 4, :]).then_inc(s_w1st[b % 4], 16)
            def root(i):
                act.wait_ge(s_rsin, i + 1)
                nc.scalar.activation(rs_root[:, :], rs_in[:, :], ACT.Sqrt).then_inc(s_root, 1)

            root(0)
            for m in range(NM):
                act.wait_ge(s_norm, m + 1)
                nc.scalar.activation(hrow[:, m, :], hrow[:, m, :], ACT.Relu).then_inc(s_h, 1)

            def high(dst, b, count):
                act.wait_ge(s_tp, count)
                nc.scalar.copy(dst, ps[:, b, :]).then_inc(s_th, 1)

            for k in range(KT):
                high(actT_h[:, k, :], k, k + 1)

            def round_w(q, k):
                act.wait_ge(s_raw[k % RAW], (q * 2 + k // RAW) * 16 + 16)
                act.wait_ge(s_slot, q * KT + k + 1)
                nc.scalar.copy(ring_h[:, k, :], raw[:, k % RAW, :]).then_inc(s_high, 1)

            def copy_a(t, n, m):
                b = n * NM + m
                chunk_done(act, t * 4 + n)
                if b >= 2:
                    act.wait_ge(s_ast[m % 2], t * 64 + (b // 2) * 16)
                nc.scalar.copy(stage[:, m % 2, :], ps[:, b, :]).then_inc(s_afree, 1)
                act.wait_ge(s_afree, t * 8 + b + 1)
                act.dma_start(tab_a[bass.ds(t * N + m * P, P), n * FB:(n + 1) * FB], stage[:, m % 2, :]).then_inc(s_ast[m % 2], 16)

            def store_b(t, n, m):
                b = n * NM + m
                if b < 2:
                    act.wait_ge(s_ast[m % 2], t * 64 + 64)
                act.wait_ge(s_bfree, t * 8 + 8 + b + 1)
                act.dma_start(tab_b[bass.ds(t * N + m * P, P), n * FB:(n + 1) * FB], stage[:, 2 + m % 2, :]).then_inc(s_bst[m % 2], 16)

            def chunk(q, n, also=None):
                for k in range(KT):
                    round_w(q, k)
                    if also and k % 2 == 1:
                        also(n, k // 2)

            for n in range(NN):
                chunk(n, n)
            with act.Fori(0, 2) as t:
                for n in range(NN):
                    chunk(t * 4 + 2 + n, n, lambda n, m: copy_a(t, n, m))
                for n in range(NN):
                    chunk(t * 4 + 4 + n, n, lambda n, m: store_b(t, n, m))
            for n in range(NN):
                chunk(10 + n, n, lambda n, m: copy_a(2, n, m))
            for n in range(NN):
                for m in range(NM):
                    store_b(2, n, m)

            q = CH_EDGE
            for c in range(4):
                chunk(q + c, c)
            q += 4
            act.wait_ge(s_edge, ET + GB)
            for m in range(NM):
                nc.scalar.copy(hrow_h[:, m, :], hrow[:, m, :]).then_inc(s_hr_h, 1)
            act.wait_ge(s_mx, 1)
            for t in range(3):
                for k in range(NM):
                    nc.scalar.activation(logit_d[:, t, k, :], logit_d[:, t, k, :], ACT.Exp,
                                         bias=nmx[:, k:k + 1]).then_inc(s_exp, 1)
            done = KT
            for k in range(NM):
                high(attT_h[:, k, :], k, done + k + 1)
            done += NM
            act.wait_ge(s_adj, 1)
            root(1)
            nc.scalar.copy(adj_h[:, :, :], adj[:, :, :]).then_inc(s_adjs, 1)
            for k in range(KT):
                high(actT_h[:, k, :], k, done + k + 1)
            done += KT
            for c in range(4):
                chunk(q + c, c)
            q += 4
            for i, (m, n) in enumerate(UPD):
                act.wait_ge(s_bsum, i + 1)
                v = topsum[:, m, n * FB:(n + 1) * FB]
                nc.scalar.activation(v, v, ACT.Relu).then_inc(s_brelu, 1)
            root(2)
            for m in range(NM):
                act.wait_ge(s_norm, NM + m + 1)
                nc.scalar.copy(hrow_h[:, m, :], topsum[:, m, :]).then_inc(s_hr_h, 1)
            for n in range(1):
                chunk(q, 0)
            for k in range(KT):
                high(actT_h[:, k, :], k, done + k + 1)
            chunk(q + 1, 1)

        @block.tensor
        def _(pe):
            pe.sem_inc(s_slot, KT)
            pe.sem_inc(s_ohu, 2)
            pe.wait_ge(s_gconst, 5)
            pe.wait_ge(s_w1row, 16)
            for b in range(NN * KT):
                n, k = b // KT, b % KT
                if b >= 8:
                    pe.wait_ge(s_w1e, b - 7)
                for o in range(4):
                    mm = nc.tensor.transpose(ps[:, b % 8, o * P:(o + 1) * P], w1row[:, n * 4 + o, k * P:(k + 1) * P], ident[:, :])
                mm.then_inc(s_w1t, 1)
            pe.wait_ge(s_w1e, NN * KT)
            pe.wait_ge(s_idxT, 1)
            for j in range(2):
                mm = nc.tensor.transpose(ps[:, 7, j * ET:(j + 1) * ET], rows_f[:, j, :], ident[0:ET, 0:ET])
            mm.then_inc(s_idxT, 1)
            pe.wait_ge(s_idxok, 1)
            pe.wait_ge(s_h, NM)
            for k in range(KT):
                for m in range(NM):
                    mm = nc.tensor.transpose(ps[:, k, m * P:(m + 1) * P], hrow[:, m, k * P:(k + 1) * P], ident[:, :])
                mm.then_inc(s_tp, 1)
            pe.wait_ge(s_tl, KT)

            def product(b, pairs):
                for i, (w, v) in enumerate(pairs):
                    mm = nc.tensor.matmul(ps[:, b, :], w, v, start=(i == 0), stop=(i == len(pairs) - 1))
                return mm

            def chunk(q, n, ms, bank_free=None):
                for k in range(KT):
                    pe.wait_ge(s_low, RAW + q * KT + k + 1)
                    for m in ms:
                        if k == 0 and bank_free:
                            bank_free(n, m)
                        for i, (w, v) in enumerate(passes(actT_h[:, k, m * P:(m + 1) * P], actT_l[:, k, m * P:(m + 1) * P],
                                                          ring_h[:, k, :], ring_l[:, k, :])):
                            mm = nc.tensor.matmul(ps[:, n * NM + m, :], w, v, start=(k == 0 and i == 0),
                                                  stop=(k == KT - 1 and i == 2))
                    mm.then_inc(s_slot, 1)

            with pe.Fori(0, 3) as t:
                for n in range(NN):
                    chunk(t * 4 + n, n, range(NM), lambda n, m: pe.wait_ge(s_bfree, t * 8 + n * NM + m + 1))
                for n in range(NN):
                    chunk(t * 4 + 2 + n, n, range(NM), lambda n, m: pe.wait_ge(s_afree, t * 8 + n * NM + m + 1))
            pe.wait_ge(s_afree, 24)
            pe.wait_ge(s_bfree, 8 + 24)

            def tile_counts(q, s, stop=False):
                pe.wait_ge(s_oh, q + 1)
                for k in range(NM):
                    c = slice(k * P, (k + 1) * P)
                    nc.tensor.matmul(ps[:, k, :], onehot[:, s, 1, c], onehot[:, s, 0, :], start=False, stop=stop, skip_group_check=True)
                    nc.tensor.matmul(ps[:, 4 + k, :], onehot[:, s, 2, c], onehot[:, s, 0, :], start=False, stop=False, skip_group_check=True)
                    mm = nc.tensor.matmul(ps[:, 4 + k, :], onehot[:, s, 3, c], onehot[:, s, 0, :], start=False, stop=stop, skip_group_check=True)
                mm.then_inc(s_ohu, 1)

            def open_banks(kind):
                if kind:
                    pe.wait_ge(s_kfree, kind)
                for b in range(8):
                    nc.tensor.matmul(ps[:, b, :], zeros_r[:, 0:P], zeros_r[:, :], start=True, stop=False, skip_group_check=True)

            q0 = 0
            for kind, tiles in enumerate((T_HO, T_HH, T_OO)):
                open_banks(kind)
                if tiles > 2:
                    with pe.Fori(0, tiles // 2 - 1) as i:
                        for s in range(2):
                            tile_counts(i * 2 + q0 + s, s)
                tile_counts(q0 + tiles - 2, 0)
                tile_counts(q0 + tiles - 1, 1, stop=True)
                q0 += tiles

            pe.wait_ge(s_kfree, 3)
            q = CH_EDGE
            for c, (_, _, n, ms) in enumerate(NODE[0]):
                chunk(q + c, n, ms)
            q += 4
            pe.wait_ge(s_top, 8)
            pe.wait_ge(s_att, 1)
            for k in range(NM):
                for m in range(NM):
                    mm = nc.tensor.transpose(ps[:, k, m * P:(m + 1) * P], logit_d[:, 0, m, k * P:(k + 1) * P], ident[:, :])
                mm.then_inc(s_tp, 1)
            pe.wait_ge(s_adj, 1)
            for m in range(NM):
                for k in range(NM):
                    mm = nc.tensor.matmul(ps[:, 4, m:m + 1], adj[:, k, m * P:(m + 1) * P], ones[:, :], start=(k == 0), stop=(k == NM - 1))
            mm.then_inc(s_deg, 1)
            pe.wait_ge(s_tl, KT + NM)
            pe.wait_ge(s_hr_l, NM)
            for f in range(KT):
                if f == NM:
                    pe.wait_ge(s_dinv, 1)
                    for m in range(NM):
                        for k in range(NM):
                            mm = nc.tensor.matmul(ps[:, 5, m:m + 1], adj[:, k, m * P:(m + 1) * P], dinv[:, k:k + 1], start=(k == 0), stop=(k == NM - 1))
                    mm.then_inc(s_deg, 1)
                if f == 5:
                    pe.wait_ge(s_dinv, 2)
                c = slice(f * P, (f + 1) * P)
                product(f, [p for k in range(NM) for p in passes(hrow_h[:, k, c], hrow_l[:, k, c], attT_h[:, k, :], attT_l[:, k, :])]
                        ).then_inc(s_tp, 1)
            pe.wait_ge(s_tl, 2 * KT + NM)
            for c, (_, _, n, ms) in enumerate(NODE[1]):
                chunk(q + c, n, ms)
            q += 4
            pe.wait_ge(s_bsum, 8)
            pe.wait_ge(s_adjs, 2)
            pe.wait_ge(s_hr_l, 2 * NM)
            for f in range(KT):
                c = slice(f * P, (f + 1) * P)
                product(f, [p for k in range(NM) for p in passes(hrow_h[:, k, c], hrow_l[:, k, c], adj_h[:, k, :], adj_l[:, k, :])]
                        ).then_inc(s_tp, 1)
            pe.wait_ge(s_tl, 3 * KT + NM)
            for c, (_, _, n, ms) in enumerate(LAST):
                chunk(q + c, n, ms)

        @block.vector
        def _(dve):
            dve.sem_inc(s_low, RAW)
            dve.sem_inc(s_bfree, 8)
            dve.sem_inc(s_edge, GB)
            chain = [0]

            def step(ins):
                chain[0] += 1
                ins.then_inc(s_v, 1)
                dve.wait_ge(s_v, chain[0])

            f32 = lambda ap: ap.bitcast(F32)

            dve.wait_ge(s_idx, 64)
            nc.vector.tensor_copy(rows_f[:, :, :], rows_i[:, :, :]).then_inc(s_idxT, 1)
            dve.wait_ge(s_idxT, 2)
            step(nc.vector.tensor_copy(node_f[:, :, :].rearrange("p t j -> p j t"),
                                       ps[:, 7, 0:2 * ET].rearrange("p (j t) -> p j t", j=2)))
            for a, b, t in ((0, T_HO, 0), (T_HO, T_HO + T_HH, 2), (T_HO + T_HH, ET, 1)):
                step(nc.vector.tensor_scalar(tabl_f[:, a:b, :], node_f[:, a:b, :], float(t * N), None, ALU.add))
            nc.vector.tensor_copy(tabl_i[:, :, :], tabl_f[:, :, :]).then_inc(s_idxok, 1)

            roots = [0]

            def rsqrt(out, val):
                roots[0] += 1
                nc.vector.tensor_copy(rs_in[:, :], val).then_inc(s_rsin, 1)
                dve.wait_ge(s_rsin, roots[0])
                dve.wait_ge(s_root, roots[0])
                step(nc.vector.reciprocal(out, rs_root[:, :]))
                step(nc.vector.tensor_tensor(rs_t[:, :], out, out, ALU.mult))
                step(nc.vector.tensor_tensor(rs_t[:, :], rs_t[:, :], rs_in[:, :], ALU.mult))
                step(nc.vector.tensor_scalar(rs_t[:, :], rs_t[:, :], -0.5, 1.5, ALU.mult, ALU.add))
                return nc.vector.tensor_tensor(out, out, rs_t[:, :], ALU.mult)

            def row_stats(m, row):
                for i in range(2):
                    ins = nc.vector.bn_stats(stats[:, m, i, :], row[:, i * FB:(i + 1) * FB])
                step(ins)
                step(nc.vector.bn_aggr(mv[:, m, :], stats[:, m, :, :].rearrange("p a b -> p (a b)")))

            def row_scales():
                step(nc.vector.tensor_scalar(var_e[:, :], mv[:, :, 1], EPS, None, ALU.add))
                step(rsqrt(rstd[:, :], var_e[:, :]))

            def norm(m, src_row, dst_row):
                return nc.vector.tensor_scalar(dst_row, src_row, mv[:, m, 0:1], rstd[:, m:m + 1], ALU.subtract, ALU.mult)

            for m in range(NM):
                dve.wait_ge(s_x[m], 16)
                row_stats(m, gath_a[:, m, :])
            row_scales()
            for m in range(NM):
                norm(m, gath_a[:, m, :], hrow[:, m, :]).then_inc(s_norm, 1)

            def low(dst, high, b, count):
                dve.wait_ge(s_th, count)
                nc.vector.tensor_tensor(dst, ps[:, b, :], f32(high), ALU.subtract).then_inc(s_tl, 1)

            for k in range(KT):
                low(actT_l[:, k, :], actT_h[:, k, :], k, k + 1)

            def low_w(q, k):
                dve.wait_ge(s_high, q * KT + k + 1)
                nc.vector.tensor_tensor(ring_l[:, k, :], raw[:, k % RAW, :], f32(ring_h[:, k, :]), ALU.subtract).then_inc(s_low, 1)

            def copy_b(t, n, m):
                b = n * NM + m
                chunk_done(dve, t * 4 + 2 + n)
                if 8 * t + b >= 2:
                    dve.wait_ge(s_bst[m % 2], t * 64 + (b // 2) * 16)
                nc.vector.tensor_tensor(stage[:, 2 + m % 2, :], ps[:, b, :], bias3[:, t, n * FB:(n + 1) * FB], ALU.add).then_inc(s_bfree, 1)

            def edge(q, s, u):
                dve.wait_ge(s_g[s], u * 32 + 32)
                nc.vector.tensor_tensor(gath_a[:, s, :], gath_a[:, s, :], gath_b[:, s, :], ALU.add).then_inc(s_esum, 1)
                dve.wait_ge(s_esum, q + 1)
                nc.vector.scalar_tensor_tensor(out=gath_b[:, s, :], in0=gath_a[:, s, :], scalar=0.0, in1=wa_b[:, :],
                                               op0=ALU.max, op1=ALU.mult, accum_out=lg[:, bass.ds(q, 1)]).then_inc(s_edge, 1)

            with dve.Fori(0, 4) as q:
                for k in range(KT):
                    low_w(q, k)
            dve.wait_ge(s_bias, 48)
            for n in range(NN):
                for k in range(KT):
                    low_w(4 + n, k)
                    if k % 2:
                        copy_b(0, n, k // 2)
            dve.wait_ge(s_const, 32)
            for j, q0 in enumerate((6, 8, 10)):
                for n in range(NN):
                    for k in range(KT):
                        low_w(q0 + n, k)
                        e = (2 * j + n) * KT + k
                        edge(e, e % GB, e // GB)
                        if j == 1 and k % 2:
                            copy_b(1, n, k // 2)
            for n in range(NN):
                for m in range(NM):
                    copy_b(2, n, m)
            for k in range(KT):
                low_w(CH_EDGE, k)
            for e in range(6 * KT, T_HO):
                edge(e, e % GB, e // GB)

            def split_logits(a, b):
                dve.wait_ge(s_edge, GB + b)
                step(nc.vector.tensor_scalar(lgb[:, a:b], lg[:, a:b], ba[:, 0:1], None, ALU.add))
                step(nc.vector.tensor_copy(lgh[:, a:b], lgb[:, a:b]))
                step(nc.vector.tensor_tensor(lgl[:, a:b], lgb[:, a:b], f32(lgh[:, a:b]), ALU.subtract))

            def onehots(q, s):
                dve.wait_ge(s_ohu, q + 1)
                c = bass.ds(q, 1)
                nc.vector.tensor_scalar(onehot[:, s, 0, :], iota_f[:, :], node_f[:, c, 0], None, ALU.is_equal)
                nc.vector.tensor_scalar(onehot[:, s, 1, :], iota_f[:, :], node_f[:, c, 1], None, ALU.is_equal)
                nc.vector.tensor_scalar(onehot[:, s, 2, :], iota_f[:, :], node_f[:, c, 1], f32(lgh[:, c]), ALU.is_equal, ALU.mult)
                nc.vector.tensor_scalar(onehot[:, s, 3, :], iota_f[:, :], node_f[:, c, 1], lgl[:, c], ALU.is_equal, ALU.mult).then_inc(s_oh, 1)

            def copy_kind(order, t):
                dve.wait_ge(s_ohu, 2 + (T_HO, T_HO + T_HH, ET)[order])
                step(nc.vector.tensor_copy(count_d[:, t, :, :], ps[:, 0:4, :]))
                step(nc.vector.tensor_scalar(adj[:, :, :], count_d[:, t, :, :], 1.0, None, ALU.max))
                step(nc.vector.reciprocal(adj[:, :, :], adj[:, :, :]))
                nc.vector.tensor_tensor(logit_d[:, t, :, :], ps[:, 4:8, :], adj[:, :, :], ALU.mult).then_inc(s_kfree, 1)
                dve.wait_ge(s_kfree, order + 1)
                step(nc.vector.tensor_scalar(adj[:, :, :], count_d[:, t, :, :], 0.0, -BIG, ALU.is_equal, ALU.mult))
                step(nc.vector.tensor_tensor(logit_d[:, t, :, :], logit_d[:, t, :, :], adj[:, :, :], ALU.add))
                step(nc.vector.tensor_reduce(mx3[:, t, :], logit_d[:, t, :, :], AX.X, ALU.max))

            split_logits(0, T_HO)
            with dve.Fori(0, 3) as i:
                for u in range(4):
                    edge(i * 4 + T_HO + u, u, i + T_HO // GB)
                    for v in range(4):
                        onehots(i * 16 + u * 4 + v, v % 2)
            for q in range(48, T_HO):
                onehots(q, q % 2)
            for i in range(2):
                dve.wait_ge(s_ast[i], 16 * 12)
                dve.wait_ge(s_bst[i], 16 * 12)
            split_logits(T_HO, ET)
            copy_kind(0, 0)
            for q in range(T_HO, T_HO + T_HH):
                onehots(q, q % 2)
            copy_kind(1, 2)
            with dve.Fori(0, T_OO // 2) as i:
                for s in range(2):
                    onehots(i * 2 + T_HO + T_HH + s, s)
            copy_kind(2, 1)

            step(nc.vector.tensor_tensor(mx[:, :], mx3[:, 0, :], mx3[:, 1, :], ALU.max))
            step(nc.vector.tensor_tensor(mx[:, :], mx[:, :], mx3[:, 2, :], ALU.max))
            nc.vector.tensor_scalar(nmx[:, :], mx[:, :], -1.0, None, ALU.mult).then_inc(s_mx, 1)
            q = CH_EDGE
            for c in range(1, 4):
                for k in range(KT):
                    low_w(q + c, k)
            q += 4
            step(nc.vector.tensor_tensor(adj[:, :, :], count_d[:, 0, :, :], count_d[:, 1, :, :], ALU.add))
            step(nc.vector.tensor_tensor(adj[:, :, :], adj[:, :, :], count_d[:, 2, :, :], ALU.add))
            for k in range(NM):
                ins = nc.vector.scalar_tensor_tensor(out=adj[:, k, :], in0=iota_f[:, :], scalar=rowid[:, k:k + 1],
                                                     in1=adj[:, k, :], op0=ALU.is_equal, op1=ALU.add)
            ins.then_inc(s_adj, 1)
            for t in range(3):
                dve.wait_ge(s_exp, NM * (t + 1))
                ins = nc.vector.tensor_tensor(logit_d[:, t, :, :], logit_d[:, t, :, :], count_d[:, t, :, :], ALU.mult)
                if t:
                    step(ins)
                    step(nc.vector.tensor_tensor(logit_d[:, 0, :, :], logit_d[:, 0, :, :], logit_d[:, t, :, :], ALU.add))
            step(nc.vector.tensor_reduce(den[:, :], logit_d[:, 0, :, :], AX.X, ALU.add))
            step(nc.vector.tensor_scalar(den[:, :], den[:, :], 1e-30, None, ALU.max))
            step(nc.vector.reciprocal(rden[:, :], den[:, :]))
            for k in range(NM):
                ins = nc.vector.tensor_scalar(logit_d[:, 0, k, :], logit_d[:, 0, k, :], rden[:, k:k + 1], None, ALU.mult)
            ins.then_inc(s_att, 1)
            dve.wait_ge(s_hr_h, NM)
            for m in range(NM):
                nc.vector.tensor_tensor(hrow_l[:, m, :], hrow[:, m, :], f32(hrow_h[:, m, :]), ALU.subtract).then_inc(s_hr_l, 1)
            dve.wait_ge(s_bias2, 48)
            for i, (m, n) in enumerate(UPD):
                chunk_done(dve, CH_EDGE + UPD_CHUNK[i])
                c = slice(n * FB, (n + 1) * FB)
                nc.vector.tensor_tensor(topsum[:, m, c], ps[:, n * NM + m, :], bias3[:, 0 if m == 0 else 1, c], ALU.add).then_inc(s_top, 1)
            done = KT
            for k in range(NM):
                low(attT_l[:, k, :], attT_h[:, k, :], k, done + k + 1)
            done += NM
            dve.wait_ge(s_deg, 1)
            rsqrt(dinv[:, :], ps[:, 4, 0:NM]).then_inc(s_dinv, 1)
            dve.wait_ge(s_adjs, 1)
            nc.vector.tensor_tensor(adj_l[:, :, :], adj[:, :, :], f32(adj_h[:, :, :]), ALU.subtract).then_inc(s_adjs, 1)
            for k in range(KT):
                if k == NM:
                    dve.wait_ge(s_deg, 2)
                    nc.vector.tensor_copy(wrow[:, :], ps[:, 5, 0:NM]).then_inc(s_dinv, 1)
                low(actT_l[:, k, :], actT_h[:, k, :], k, done + k + 1)
            done += KT
            for c in range(4):
                for k in range(KT):
                    low_w(q + c, k)
            for i, (m, n) in enumerate(UPD):
                chunk_done(dve, q + UPD_CHUNK[i])
                c = slice(n * FB, (n + 1) * FB)
                nc.vector.tensor_tensor(topsum[:, m, c], topsum[:, m, c], ps[:, n * NM + m, :], ALU.add).then_inc(s_bsum, 1)
            q += 4
            for i, (m, n) in enumerate(UPD):
                dve.wait_ge(s_brelu, i + 1)
                dve.wait_ge(s_xr[m], 16)
                c = slice(n * FB, (n + 1) * FB)
                nc.vector.tensor_tensor(hrow[:, m, c], hrow[:, m, c], topsum[:, m, c], ALU.add).then_inc(s_x1, 1)
            dve.wait_ge(s_x1, 8)
            dve.wait_ge(s_dinv, 2)
            for m in range(NM):
                row_stats(m, hrow[:, m, :])
            row_scales()
            for m in range(NM):
                step(norm(m, hrow[:, m, :], topsum[:, m, :]))
                nc.vector.tensor_scalar(topsum[:, m, :], topsum[:, m, :], 0.0, dinv[:, m:m + 1], ALU.max, ALU.mult).then_inc(s_norm, 1)
            for m in range(NM):
                dve.wait_ge(s_hr_h, NM + m + 1)
                nc.vector.tensor_tensor(hrow_l[:, m, :], topsum[:, m, :], f32(hrow_h[:, m, :]), ALU.subtract).then_inc(s_hr_l, 1)
            for k in range(KT):
                low_w(q, k)
            for k in range(KT):
                low(actT_l[:, k, :], actT_h[:, k, :], k, done + k + 1)
            for k in range(KT):
                low_w(q + 1, k)
            for n in range(NN):
                c = slice(n * FB, (n + 1) * FB)
                chunk_done(dve, q + n)
                for m in range(NM):
                    step(nc.vector.scalar_tensor_tensor(out=topsum[:, m, c], in0=bias3[:, 2, c], scalar=wrow[:, m:m + 1],
                                                        in1=ps[:, n * NM + m, :], op0=ALU.mult, op1=ALU.add))
                    nc.vector.scalar_tensor_tensor(out=topsum[:, m, c], in0=topsum[:, m, c], scalar=dinv[:, m:m + 1],
                                                   in1=hrow[:, m, c], op0=ALU.mult, op1=ALU.add).then_inc(s_out, 1)


_INS = ['x', 'src', 'dst', 'L0_gnn_W_hh', 'L0_gnn_b_hh', 'L0_gnn_W_oo', 'L0_gnn_b_oo', 'L0_gnn_W_ho', 'L0_gnn_b_ho',
        'L0_gnn_W_a', 'L0_gnn_b_a', 'L0_gnn_W_hn', 'L0_gnn_b_hn', 'L0_gnn_W_on', 'L0_gnn_b_on', 'L1_gnn_W', 'L1_gnn_b']


def kernel(**inputs):
    import numpy as _np
    import concourse.bacc as _bacc
    from concourse import mybir as _mybir
    from concourse.bass_utils import run_bass_kernel_spmd as _run

    nc = _bacc.Bacc("TRN2", target_bir_lowering=False, num_devices=1)
    arrays, args = {}, []
    for name in _INS:
        a = _np.ascontiguousarray(inputs[name])
        arrays[f"in_{name}_dram"] = a
        args.append(nc.dram_tensor(f"in_{name}_dram", a.shape, _mybir.dt.from_np(a.dtype), kind="ExternalInput").ap())
    out = nc.dram_tensor("out_dram", inputs['x'].shape, _mybir.dt.float32, kind="ExternalOutput").ap()
    gnn_kernel(nc, *args, out)
    r = _run(nc, [arrays], core_ids=[0])
    return r.results[0]["out_dram"]
```

```python
from contextlib import ExitStack

import concourse.bass as bass
from concourse import mybir

P = 128
FB = 512
KB = 1024
ALU = mybir.AluOpType
ACT = mybir.ActivationFunctionType
AX = mybir.AxisListType
F32 = mybir.dt.float32
F32R = mybir.dt.float32r
U16 = mybir.dt.uint16
BF16 = mybir.dt.bfloat16
FP16 = mybir.dt.float16
I32 = mybir.dt.int32
U32 = mybir.dt.uint32

E_HH, E_OO = 256, 1280
NH = 128
EPS = 1e-5
BIG = 1e30


def gnn_kernel(nc, x, src, dst, W_hh, b_hh, W_oo, b_oo, W_ho, b_ho, W_a, b_a,
               W_hn, b_hn, W_on, b_on, W1, b1, out):
    N, D = x.shape
    E = src.shape[0]
    NM = N // P
    KT = D // P
    NN = D // FB
    ET = E // P
    T_HH, T_OO = E_HH // P, E_OO // P
    T_HO = ET - T_HH - T_OO
    EARLY = T_HH + T_OO
    assert NM == 4 and KT == 8 and NN == 2 and N == FB and NH == P

    with ExitStack() as ctx:
        def sem(name):
            return ctx.enter_context(nc.semaphore(name))

        BASE = 16512
        assert BASE >= nc.sbuf_base
        at = {}

        def sb(name, shape, dt, size=None, over=None, shift=0):
            width = mybir.dt.size(dt)
            for n in shape[1:]:
                width *= n
            if over is None:
                off = at.get("end", BASE)
                at["end"] = off + -(-(size or width) // 32) * 32
            else:
                off = at[over] + shift
            at[name] = off
            return nc.alloc_sbuf_tensor_at(name, shape, dt, offset=off)

        actT_h = sb("actT_h", [P, KT, N], F32R)
        actT_l = sb("actT_l", [P, KT, N], F32R)
        hrow = sb("hrow", [P, NM, D], F32)
        ring_h = sb("ring_h", [P, KT, FB], F32R)
        ring_l = sb("ring_l", [P, KT, FB], F32R)
        RAW = 4
        raw = sb("raw", [P, RAW, FB], F32)
        GB = 8
        gath = sb("gath", [P, GB, D], F32)
        logit_d = sb("logit_d", [P, 3, NM, N], F32)
        count_d = sb("count_d", [P, 3, NM, N], U16)
        OS = 4
        G = 8
        topsum = sb("topsum", [P, NM, D], F32)
        onehot = sb("onehot", [P, OS, 4, N], BF16, over="topsum")
        stage = sb("stage", [P, 4, FB], F32)
        bias3 = sb("bias3", [P, 3, D], F32)
        wa_b = sb("wa_b", [P, D], F32)
        iota_f = sb("iota_f", [P, N], FP16)
        ident = sb("ident", [P, P], F32)
        zeros_r = sb("zeros_r", [P, N], BF16)
        rows_i = sb("rows_i", [ET, 2, P], I32, over="logit_d")
        rows_f = sb("rows_f", [ET, 3, P], F32, over="logit_d", shift=8 * P)
        span = sb("span", [ET, 2], F32)
        span_b = sb("span_b", [ET, 2], F32)
        base = sb("base", [ET, 1], F32)
        code = sb("code", [ET, 1], F32)
        pow8 = sb("pow8", [1, ET // G, G], F32)
        code_row = sb("code_row", [1, ET // G, G], F32)
        pack_f = sb("pack_f", [1, ET // G], F32)
        pack_i = sb("pack_i", [1, ET // G], I32)
        node_f = sb("node_f", [P, ET, 3], F32)
        tabl_f = sb("tabl_f", [P, ET, 2], F32, over="logit_d", shift=20 * P)
        tabl_i = sb("tabl_i", [P, ET, 2], U32)
        tabl_s = sb("tabl_s", [P, GB, 2], U32)
        lg = sb("lg", [P, ET], F32)
        lgb = sb("lgb", [P, ET], F32)
        lgr = sb("lgr", [P, ET], F32)
        lgp = sb("lgp", [P, 3, ET], BF16)
        lgs = sb("lgs", [P, 3, ET], F32)
        ba = sb("ba", [P, 1], F32)
        stats = sb("stats", [P, NM, 2, 6], F32)
        mv = sb("mv", [P, NM, 2], F32)
        rstd = sb("rstd", [P, NM], F32)
        mx3 = sb("mx3", [P, 3, NM], F32)
        mx = sb("mx", [P, NM], F32)
        nmx = sb("nmx", [P, NM], F32)
        den = sb("den", [P, NM], F32)
        rden = sb("rden", [P, NM], F32)
        rowid = sb("rowid", [P, NM], F32)
        ones = sb("ones", [P, 1], F32)
        var_e = sb("var_e", [P, NM], F32)
        rs_in = sb("rs_in", [P, NM], F32)
        rs_root = sb("rs_root", [P, NM], F32)
        rs_t = sb("rs_t", [P, NM], F32)
        dinv = sb("dinv", [P, NM], F32)
        wrow = sb("wrow", [P, NM], F32)
        assert at["end"] <= nc.sbuf_usable_end, at["end"] - nc.sbuf_usable_end

        hrow_h = sb("hrow_h", [P, NM, D], F32R, over="gath")
        hrow_l = sb("hrow_l", [P, NM, D], F32R, over="gath", shift=4 * NM * D)
        w1row = sb("w1row", [P, 4, D], F32, over="logit_d", shift=4 * NM * N)
        attT_h = sb("attT_h", [P, NM, N], F32R, over="logit_d", shift=4 * NM * N)
        attT_l = sb("attT_l", [P, NM, N], F32R, over="logit_d", shift=8 * NM * N)
        mask = sb("mask", [P, NM, N], F32, over="gath", shift=4 * NM * D)
        adj = sb("adj", [P, NM, N], F32, over="stage")
        adj_h = sb("adj_h", [P, NM, N], F32R, over="logit_d")
        adj_l = sb("adj_l", [P, NM, N], F32R, over="count_d")

        ps = ctx.enter_context(nc.psum_tensor("ps", [P, 8, FB], F32))
        tab_a = nc.dram_tensor("tab_a", [3 * N, D], F32).ap()
        tab_b = nc.dram_tensor("tab_b", [3 * N, D], F32).ap()
        top_d = nc.dram_tensor("top_d", [N, D], F32).ap()

        s_x = [sem(f"x_loaded{m}") for m in range(NM)]
        s_idx = sem("edges_loaded")
        s_const = sem("consts_loaded")
        s_bias = sem("bias_loaded")
        s_bias2 = sem("bias2_loaded")
        s_w1row = sem("w1_loaded")
        s_raw = [sem(f"raw_loaded{i}") for i in range(RAW)]
        s_high = sem("w_high_ready")
        s_low = sem("w_low_ready")
        s_slot = sem("w_slots_free")
        s_bank = sem("table_banks_done")
        s_copied = sem("table_banks_free")
        s_st = [sem(f"stage_stored{i}") for i in range(4)]
        s_topl = [sem(f"top_loaded{m}") for m in range(NM)]
        s_part = sem("onehot_parts_ready")
        s_pool = sem("pool_chain")
        s_gconst = sem("consts_made")
        s_v = sem("vector_chain")
        s_rsin = sem("rsqrt_input")
        s_root = sem("square_roots")
        s_h = sem("h_rows")
        s_norm = sem("h_normed")
        s_tp = sem("transposed_banks")
        s_th = sem("transposed_high")
        s_tl = sem("transposed_low")
        s_idxT = sem("edges_transposed")
        s_spanok = sem("edge_blocks_ready")
        s_idxok = sem("edges_ready")
        s_ga = [sem(f"gathered_src{i}") for i in range(GB)]
        s_g = [sem(f"gathered{i}") for i in range(GB)]
        s_cdone = sem("counts_ready")
        s_ccopy = sem("counts_copied")
        s_edge = sem("gather_slots_free")
        s_stg = sem("index_staged")
        s_seen = sem("index_seen")
        s_oh = sem("onehots_ready")
        s_ohu = sem("onehot_slots_free")
        s_kind = sem("kind_counted")
        s_kfree = sem("kind_banks_free")
        s_mx = sem("row_max_ready")
        s_exp = sem("exp_done")
        s_att = sem("attention_ready")
        s_top = sem("top_banks_free")
        s_hr_h = sem("rows_high")
        s_hr_l = sem("rows_low")
        s_xr = [sem(f"residual_loaded{m}") for m in range(NM)]
        s_bsum = sem("update_summed")
        s_brelu = sem("update_relu")
        s_x1 = sem("x1_ready")
        s_adj = sem("adj_ready")
        s_adjs = sem("adj_split")
        s_deg = sem("deg_banks")
        s_dinv = sem("dinv_ready")
        s_out = sem("out_rows")
        s_outst = [sem(f"out_stored{i}") for i in range(2 * NM)]


        def passes(hi, lo, mh, ml):
            return ((hi, mh), (hi, ml), (lo, mh))

        block = ctx.enter_context(nc.Block())

        KINDS = ((W_ho, b_ho), (W_oo, b_oo), (W_hh, b_hh))
        TILES = (T_HO, T_OO, T_HH)
        CH_EDGE = 3 * 2 * NN
        NODE = [[(w, r, n, ms) for w, ms in halves for n in range(NN)]
                for r, halves in ((0, ((W_on, (1, 2, 3)), (W_hn, (0,)))), (D, ((W_hn, (0,)), (W_on, (1, 2, 3)))))]
        TOP = [(m, n) for _, _, n, ms in NODE[0] for m in ms]
        TP_H = KT
        TP_ATT = TP_H + NM
        TP_Z = TP_ATT + KT
        TP_W1 = TP_Z + KT
        TP_G = TP_W1 + KT

        @block.sync
        def _(sp):
            for m in range(NM):
                sp.dma_start(gath[:, m, :], x[m * P:(m + 1) * P, :]).then_inc(s_x[m], 16)

            def load(w, row, n, q, k):
                sp.wait_ge(s_low, q * KT + k + 1)
                sp.dma_start(raw[:, k % RAW, :], w[bass.ds(row + k * P, P), n * FB:(n + 1) * FB]).then_inc(s_raw[k % RAW], 16)

            for t, (w, _) in enumerate(KINDS):
                with sp.Fori(0, 2) as half:
                    for n in range(NN):
                        for k in range(KT):
                            load(w, half * D, n, (half * NN + n) + t * 2 * NN, k)
            q = CH_EDGE
            for w, row, n, _ in NODE[0] + NODE[1]:
                for k in range(KT):
                    load(w, row, n, q, k)
                q += 1
            for n in range(NN):
                sp.wait_ge(s_tp, TP_Z if n == 0 else TP_W1)
                sp.dma_start(w1row[:, :, :], W1[n * FB:(n + 1) * FB, :].rearrange("(o p) i -> p o i", p=P)).then_inc(s_w1row, 16)
            for n in range(NN):
                for m in range(NM):
                    i = n * NM + m
                    sp.wait_ge(s_out, i + 1)
                    sp.dma_start(out[m * P:(m + 1) * P, n * FB:(n + 1) * FB], topsum[:, m, n * FB:(n + 1) * FB]).then_inc(s_outst[i], 16)
            for i in range(2 * NM):
                sp.wait_ge(s_outst[i], 16)

        @block.gpsimd
        def _(pool):
            for j, e in enumerate((src, dst)):
                rows = e.rearrange("(t p) -> t p", p=P)
                to = 0
                for first, n in ((EARLY, T_HO), (T_HH, T_OO), (0, T_HH)):
                    pool.dma_start(rows_i[to:to + n, j, :], rows[first:first + n, :]).then_inc(s_idx, 16)
                    to += n
            nc.gpsimd.iota(iota_f[:, :], [[1, N]], base=0, channel_multiplier=0,
                           allow_small_or_imprecise_dtypes=True).then_inc(s_gconst, 1)
            nc.gpsimd.memset(zeros_r[:, :], 0.0).then_inc(s_gconst, 1)
            nc.gpsimd.memset(ident[:, :], 0.0).then_inc(s_pool, 1)
            pool.wait_ge(s_pool, 1)
            nc.gpsimd.affine_select(out=ident[:, :], in_=ident[:, :], compare_op=ALU.not_equal, fill=1.0,
                                    base=0, pattern=[[-1, P]], channel_multiplier=1).then_inc(s_gconst, 1)
            nc.gpsimd.iota(rowid[:, :], [[P, NM]], base=0, channel_multiplier=1,
                           allow_small_or_imprecise_dtypes=True).then_inc(s_gconst, 1)
            for j in range(G):
                nc.gpsimd.memset(pow8[:, :, j], float(8 ** j)).then_inc(s_gconst, 1)
            nc.gpsimd.memset(ones[:, :], 1.0).then_inc(s_gconst, 1)
            for m in range(NM):
                pool.wait_ge(s_x[m], 16)
            pool.dma_start(wa_b[:, :], W_a.rearrange("d a -> a d").partition_broadcast(P)).then_inc(s_const, 16)
            pool.dma_start(ba[:, :], b_a.rearrange("(a d) -> a d", a=1).partition_broadcast(P)).then_inc(s_const, 16)
            for t, (_, b) in enumerate(KINDS):
                pool.dma_start(bias3[:, t, :], b.rearrange("(a d) -> a d", a=1).partition_broadcast(P)).then_inc(s_bias, 16)

            pool.wait_ge(s_idxok, 1)

            def gather_src(q, s, kinds):
                pool.wait_ge(s_edge, q + 1)
                nc.gpsimd.tensor_copy(tabl_s[:, s, :], tabl_i[:, bass.ds(q, 1), :].rearrange("p a b -> p (a b)")).then_inc(s_stg, 1)
                pool.wait_ge(s_stg, q + 1)
                pool.sem_inc(s_seen, 1)
                pool.indirect_dma_start(out=gath[:, s, :], out_offset=None, in_=tab_a[0:kinds * N, :],
                                        in_offset=bass.IndirectOffsetOnAxis(ap=tabl_s[:, s, 0:1], axis=0)).then_inc(s_ga[s], 16)

            def gather_dst(s, u, kinds):
                pool.wait_ge(s_ga[s], u * 16 + 16)
                pool.sem_inc(s_seen, 1)
                pool.indirect_dma_start(out=gath[:, s, :], out_offset=None, in_=tab_b[0:kinds * N, :],
                                        in_offset=bass.IndirectOffsetOnAxis(ap=tabl_s[:, s, 1:2], axis=0),
                                        compute_op=ALU.add).then_inc(s_g[s], 16)

            def tables_landed(kinds):
                for i in range(4):
                    pool.wait_ge(s_st[i], 64 * kinds)

            def gather_run(first, end, kinds, pending=0):
                for q in range(first, end):
                    gather_src(q, q % GB, kinds)
                    if q - LAG >= first - pending:
                        gather_dst((q - LAG) % GB, (q - LAG) // GB, kinds)

            def gather_rest(end, kinds):
                for q in range(end - LAG, end):
                    gather_dst(q % GB, q // GB, kinds)

            LAG = 3
            tables_landed(1)
            gather_run(0, GB, 1)
            with pool.Fori(1, T_HO // GB) as i:
                for s in range(GB):
                    gather_src(i * GB + s, s, 1)
                    gather_dst((s - LAG) % GB, i if s >= LAG else i - 1, 1)
            gather_run(T_HO // GB * GB, T_HO, 1, LAG)
            gather_rest(T_HO, 1)
            tables_landed(2)
            gather_run(T_HO, T_HO + T_OO, 2)
            gather_rest(T_HO + T_OO, 2)
            tables_landed(3)
            for q in range(T_HO + T_OO, ET):
                gather_src(q, q % GB, 3)
            for q in range(T_HO + T_OO, ET):
                gather_dst(q % GB, q // GB, 3)
            pool.wait_ge(s_copied, NM + NM * CH_EDGE)
            for t, b in enumerate((b_hn, b_on, b1)):
                pool.dma_start(bias3[:, t, :], b.rearrange("(a d) -> a d", a=1).partition_broadcast(P)).then_inc(s_bias2, 16)
            pool.wait_ge(s_ohu, OS + 2 * ET)
            for i in range(4):
                pool.wait_ge(s_st[i], 16 * (CH_EDGE + 2))
            for m in range(NM):
                pool.dma_start(topsum[:, m, :], top_d[m * P:(m + 1) * P, :]).then_inc(s_topl[m], 16)
            pool.wait_ge(s_hr_l, NM)
            for m in range(NM):
                pool.dma_start(hrow[:, m, :], x[m * P:(m + 1) * P, :]).then_inc(s_xr[m], 16)

        UPD = [(0, 0), (0, 1), (1, 0), (2, 0), (3, 0), (1, 1), (2, 1), (3, 1)]
        UPD_CHUNK = [0, 1, 2, 2, 2, 3, 3, 3]

        def chunk_done(eng, q):
            eng.wait_ge(s_slot, KT + q * KT + KT)

        def bank_done(eng, q, m):
            if m < NM - 1:
                eng.wait_ge(s_bank, q * (NM - 1) + m + 1)
            else:
                chunk_done(eng, q)

        def is_a(q):
            return q // NN % 2 == 0

        @block.scalar
        def _(act):
            def root(i):
                act.wait_ge(s_rsin, i + 1)
                nc.scalar.activation(rs_root[:, :], rs_in[:, :], ACT.Sqrt).then_inc(s_root, 1)

            root(0)
            for m in range(NM):
                act.wait_ge(s_norm, m + 1)
                nc.scalar.activation(hrow[:, m, :], hrow[:, m, :], ACT.Relu).then_inc(s_h, 1)

            def high(dst, b, count):
                act.wait_ge(s_tp, count)
                nc.scalar.copy(dst, ps[:, b, :]).then_inc(s_th, 1)

            for k in range(KT):
                high(actT_h[:, k, :], k, k + 1)

            def round_w(q, k):
                act.wait_ge(s_raw[k % RAW], (q * 2 + k // RAW) * 16 + 16)
                act.wait_ge(s_slot, q * KT + k + 1)
                nc.scalar.copy(ring_h[:, k, :], raw[:, k % RAW, :]).then_inc(s_high, 1)

            def counts(t):
                act.wait_ge(s_cdone, t + 1)
                nc.scalar.copy(count_d[:, t, :, :], ps[:, 0:NM, :]).then_inc(s_ccopy, 1)

            def table(q, m):
                n, r = q % NN, q // 4 * N + m * P
                return (tab_a if is_a(q) else tab_b)[r:r + P, n * FB:(n + 1) * FB]

            def copy_a(q):
                for m in range(NM):
                    bank_done(act, q, m)
                    if q:
                        act.wait_ge(s_st[m], q * 16)
                    nc.scalar.copy(stage[:, m, :], ps[:, NM + m, :]).then_inc(s_copied, 1)
                    act.wait_ge(s_copied, NM + q * NM + m + 1)
                    act.dma_start(table(q, m), stage[:, m, :]).then_inc(s_st[m], 16)

            def store_b(q):
                for m in range(NM):
                    act.wait_ge(s_copied, NM + q * NM + m + 1)
                    act.dma_start(table(q, m), stage[:, m, :]).then_inc(s_st[m], 16)

            top_at = [0]

            def copy_top(c):
                chunk_done(act, CH_EDGE + c)
                for m in NODE[0][c][3]:
                    i = top_at[0]
                    top_at[0] += 1
                    n = NODE[0][c][2]
                    act.wait_ge(s_st[i % 4], 16 * (CH_EDGE + i // 4))
                    nc.scalar.copy(stage[:, i % 4, :], ps[:, NM + m, :]).then_inc(s_copied, 1)
                    act.wait_ge(s_copied, NM + CH_EDGE * NM + i + 1)
                    act.dma_start(top_d[m * P:(m + 1) * P, n * FB:(n + 1) * FB], stage[:, i % 4, :]).then_inc(s_st[i % 4], 16)

            def logit_parts(q):
                act.wait_ge(s_oh, ET + q + 1)
                for i in (1, 2, 0):
                    ins = nc.scalar.mul(onehot[:, q % OS, 1 + i, :], onehot[:, q % OS, 1, :], lgs[:, i, q:q + 1])
                ins.then_inc(s_part, 1)

            def chunk(q, after=None):
                for k in range(KT):
                    round_w(q, k)
                    if after:
                        after(k)

            def edge_chunk(q):
                def beside(k):
                    t = (q - 5) * G + k if q < CH_EDGE else (q - CH_EDGE) * G + k + T_HO
                    if 5 <= q and t < (T_HO if q < CH_EDGE else T_HO + T_OO):
                        logit_parts(t)
                    if k == 2 and q:
                        if q > CH_EDGE:
                            copy_top(q - 1 - CH_EDGE)
                        elif is_a(q - 1):
                            copy_a(q - 1)
                    if k == 4 and 0 < q <= CH_EDGE and not is_a(q - 1):
                        store_b(q - 1)
                    if (q, k) == (3, 3):
                        counts(0)
                    if (q, k) == (3, 7):
                        counts(1)
                    if (q, k) == (4, 1):
                        counts(2)
                    if (q, k) == (14, 5):
                        logit_parts(62)
                        logit_parts(63)
                chunk(q, beside)

            for q in range(CH_EDGE + 4):
                edge_chunk(q)
            copy_top(3)
            q = CH_EDGE + 4
            act.wait_ge(s_edge, ET + GB)
            for m in range(NM):
                nc.scalar.copy(hrow_h[:, m, :], hrow[:, m, :]).then_inc(s_hr_h, 1)
            act.wait_ge(s_mx, 1)
            for t in range(3):
                for k in range(NM):
                    nc.scalar.activation(logit_d[:, t, k, :], logit_d[:, t, k, :], ACT.Exp,
                                         bias=nmx[:, k:k + 1]).then_inc(s_exp, 1)
            for k in range(NM):
                high(attT_h[:, k, :], k, TP_H + k + 1)
            act.wait_ge(s_adj, 1)
            root(1)
            nc.scalar.copy(adj_h[:, :, :], adj[:, :, :]).then_inc(s_adjs, 1)
            for k in range(KT):
                high(actT_h[:, k, :], k, TP_ATT + k + 1)
            for c in range(4):
                chunk(q + c)
            q += 4
            for i, (m, n) in enumerate(UPD):
                act.wait_ge(s_bsum, i + 1)
                v = topsum[:, m, n * FB:(n + 1) * FB]
                nc.scalar.activation(v, v, ACT.Relu).then_inc(s_brelu, 1)

            def high_w1(q, k, b, count):
                act.wait_ge(s_tp, count)
                act.wait_ge(s_slot, q * KT + k + 1)
                nc.scalar.copy(ring_h[:, k, :], ps[:, b, :]).then_inc(s_high, 1)

            for k in range(KT):
                high_w1(q, k, k, TP_Z + k + 1)
            root(2)
            for m in range(NM):
                act.wait_ge(s_norm, NM + m + 1)
                nc.scalar.copy(hrow_h[:, m, :], topsum[:, m, :]).then_inc(s_hr_h, 1)
            for k in range(KT):
                high(actT_h[:, k, :], k, TP_W1 + k + 1)
            for k in range(KT):
                high_w1(q + 1, k, NM + k % NM, TP_G + k + 1)

        @block.tensor
        def _(pe):
            pe.sem_inc(s_slot, KT)
            pe.sem_inc(s_ohu, OS)
            pe.wait_ge(s_gconst, 5 + G)
            pe.wait_ge(s_idxT, 1)
            for j in range(3):
                nc.tensor.transpose(ps[:, 7, j * ET:(j + 1) * ET], rows_f[:, j, :], ident[0:ET, 0:ET])
            nc.tensor.transpose(ps[0:1, 6, 0:ET], code[:, :], ident[0:ET, 0:ET]).then_inc(s_idxT, 1)
            pe.wait_ge(s_spanok, 1)

            def codes(g):
                return nc.values_load_multi_w_load_instructions(
                    pack_i[0:1, bass.ds(g, 1)], engines=[mybir.EngineType.PE], min_val=0, max_val=8 ** G - 1,
                    skip_runtime_bounds_check_because="the codes are packed on the chip, 3 bits each")[1][0]

            def accumulate(code, t, s, parts):
                lo = code >> (3 * t)

                def block(j):
                    for i in range(parts):
                        mm = nc.tensor.matmul(ps[:, bass.ds((lo + j) & 3, 1), :].rearrange("p a n -> p (a n)"),
                                              onehot[:, s, 1 + i, j * P:(j + 1) * P], onehot[:, s, 0, :],
                                              start=False, stop=False, skip_group_check=True)
                    return mm

                with pe.If((lo & 4) > 0):
                    for j in range(1, NM):
                        block(j)
                block(0).then_inc(s_ohu, 1)

            def open_banks():
                for b in range(NM):
                    nc.tensor.matmul(ps[:, b, :], zeros_r[:, 0:P], zeros_r[:, :], start=True, stop=False, skip_group_check=True)

            def close_banks(done):
                for b in range(NM):
                    mm = nc.tensor.matmul(ps[:, b, :], zeros_r[:, 0:P], zeros_r[:, :], start=False, stop=True, skip_group_check=True)
                mm.then_inc(done, 1)

            pe.wait_ge(s_h, NM)
            for k in range(KT):
                for m in range(NM):
                    mm = nc.tensor.transpose(ps[:, k, m * P:(m + 1) * P], hrow[:, m, k * P:(k + 1) * P], ident[:, :])
                mm.then_inc(s_tp, 1)
            pe.wait_ge(s_tl, TP_H)

            def product(b, pairs):
                for i, (w, v) in enumerate(pairs):
                    mm = nc.tensor.matmul(ps[:, b, :], w, v, start=(i == 0), stop=(i == len(pairs) - 1))
                return mm

            def chunk(q, first, ms, bank_free=None, before=None, after=None, counted=False):
                for k in range(KT):
                    if before:
                        before(k)
                    pe.wait_ge(s_low, RAW + q * KT + k + 1)
                    for m in ms:
                        if k == 0 and bank_free:
                            bank_free(m)
                        for i, (w, v) in enumerate(passes(actT_h[:, k, m * P:(m + 1) * P], actT_l[:, k, m * P:(m + 1) * P],
                                                          ring_h[:, k, :], ring_l[:, k, :])):
                            mm = nc.tensor.matmul(ps[:, first + m, :], w, v, start=(k == 0 and i == 0),
                                                  stop=(k == KT - 1 and i == 2))
                        if counted and k == KT - 1 and m < NM - 1:
                            mm.then_inc(s_bank, 1)
                    mm.then_inc(s_slot, 1)
                    if after:
                        after(k)

            def edge_chunk(q, before=None, after=None):
                chunk(q, NM, range(NM), lambda m: pe.wait_ge(s_copied, q * NM + m + 1), before, after, counted=True)

            reg = [None]

            def count_tiles(g0, k):
                if k % 4 == 0:
                    reg[0] = codes(g0 + k // 4)
                for j in range(2):
                    t = 2 * k + j
                    pe.wait_ge(s_oh, g0 * G + t + 1)
                    accumulate(reg[0], t % G, t % OS, 1)

            def last_counts(k):
                for j in range(2):
                    t = 2 * k + j
                    q = ET - 2 * G + t
                    if q == T_HO or q == T_HO + T_OO:
                        kind = 1 if q == T_HO else 2
                        pe.wait_ge(s_ccopy, kind)
                        open_banks()
                    if t % G == 0:
                        reg[0] = codes(q // G)
                    pe.wait_ge(s_oh, q + 1)
                    accumulate(reg[0], t % G, t % OS, 1)
                    if q + 1 in (T_HO, T_HO + T_OO, ET):
                        close_banks(s_cdone)

            def add_logits(q, g, t):
                if t == 0 or reg[0] is None:
                    reg[0] = codes(g)
                pe.wait_ge(s_part, q + 1)
                accumulate(reg[0], t, t % OS, 3)

            open_banks()
            with pe.Fori(0, 3) as c:
                edge_chunk(c, after=lambda k: count_tiles(c * 2, k))
            edge_chunk(3, after=last_counts)
            edge_chunk(4)
            pe.wait_ge(s_ccopy, 3)
            open_banks()
            with pe.Fori(0, 6) as i:
                edge_chunk(i + 5, before=lambda k: add_logits(i * G + k, i, k))
            edge_chunk(11, before=lambda k: k < 4 and add_logits(48 + k, 6, k),
                       after=lambda k: k == 3 and close_banks(s_kind))

            q = CH_EDGE

            def oo_logits(k):
                if k == 0:
                    pe.wait_ge(s_kfree, 1)
                    open_banks()
                    reg[0] = None
                add_logits(T_HO + k, 6 + k // 4, (4 + k) % G)

            def last_oo_logits(k):
                if k < 2:
                    add_logits(T_HO + 8 + k, 7, 4 + k)
                if k == 1:
                    close_banks(s_kind)

            base = NM + NM * CH_EDGE
            chunk(q, NM, NODE[0][0][3], lambda m: pe.wait_ge(s_copied, NM * CH_EDGE + m + 1), oo_logits)
            chunk(q + 1, NM, NODE[0][1][3], lambda m: pe.wait_ge(s_copied, base + m), None, last_oo_logits)
            chunk(q + 2, NM, NODE[0][2][3])
            pe.wait_ge(s_kfree, 2)
            open_banks()
            reg[0] = codes(7)
            for t in (6, 7):
                add_logits(7 * G + t, 7, t)
            close_banks(s_kind)
            chunk(q + 3, NM, NODE[0][3][3], lambda m: pe.wait_ge(s_copied, base + 7))
            pe.wait_ge(s_kfree, 3)
            q += 4
            pe.wait_ge(s_att, 1)
            for k in range(NM):
                for m in range(NM):
                    mm = nc.tensor.transpose(ps[:, k, m * P:(m + 1) * P], logit_d[:, 0, m, k * P:(k + 1) * P], ident[:, :])
                mm.then_inc(s_tp, 1)
            pe.wait_ge(s_adj, 1)
            for m in range(NM):
                for k in range(NM):
                    mm = nc.tensor.matmul(ps[:, 4, m:m + 1], adj[:, k, m * P:(m + 1) * P], ones[:, :], start=(k == 0), stop=(k == NM - 1))
            mm.then_inc(s_deg, 1)
            pe.wait_ge(s_tl, TP_ATT)
            pe.wait_ge(s_hr_l, NM)
            for f in range(KT):
                if f == NM:
                    pe.wait_ge(s_dinv, 1)
                    for m in range(NM):
                        for k in range(NM):
                            mm = nc.tensor.matmul(ps[:, 5, m:m + 1], adj[:, k, m * P:(m + 1) * P], dinv[:, k:k + 1], start=(k == 0), stop=(k == NM - 1))
                    mm.then_inc(s_deg, 1)
                if f == 5:
                    pe.wait_ge(s_dinv, 2)
                c = slice(f * P, (f + 1) * P)
                product(f, [p for k in range(NM) for p in passes(hrow_h[:, k, c], hrow_l[:, k, c], attT_h[:, k, :], attT_l[:, k, :])]
                        ).then_inc(s_tp, 1)
            pe.wait_ge(s_tl, TP_Z)
            for c, (_, _, n, ms) in enumerate(NODE[1]):
                chunk(q + c, n * NM, ms)
            q += 4

            def w1_transposed(k, b):
                for o in range(4):
                    mm = nc.tensor.transpose(ps[:, b, o * P:(o + 1) * P], w1row[:, o, k * P:(k + 1) * P], ident[:, :])
                mm.then_inc(s_tp, 1)

            pe.wait_ge(s_w1row, 16)
            pe.wait_ge(s_bsum, 8)
            for k in range(KT):
                w1_transposed(k, k)
            pe.wait_ge(s_adjs, 2)
            pe.wait_ge(s_hr_l, 2 * NM)
            for f in range(KT):
                c = slice(f * P, (f + 1) * P)
                pe.wait_ge(s_low, RAW + q * KT + f + 1)
                product(f, [p for k in range(NM) for p in passes(hrow_h[:, k, c], hrow_l[:, k, c], adj_h[:, k, :], adj_l[:, k, :])]
                        ).then_inc(s_tp, 1)
            pe.wait_ge(s_w1row, 32)
            for k in range(NM):
                pe.wait_ge(s_tl, TP_Z + NM + k + 1)
                w1_transposed(k, NM + k)
            pe.wait_ge(s_tl, TP_Z + KT)
            chunk(q, 0, range(NM))
            for k in range(NM, KT):
                pe.wait_ge(s_low, RAW + (q + 1) * KT + k - NM + 1)
                w1_transposed(k, k)
            chunk(q + 1, 0, range(NM), lambda m: pe.wait_ge(s_out, m + 1))

        @block.vector
        def _(dve):
            dve.sem_inc(s_low, RAW)
            dve.sem_inc(s_copied, NM)
            dve.sem_inc(s_edge, GB)
            chain = [0]

            def step(ins):
                chain[0] += 1
                ins.then_inc(s_v, 1)
                dve.wait_ge(s_v, chain[0])

            f32 = lambda ap: ap.bitcast(F32)

            dve.wait_ge(s_idx, 96)
            step(nc.vector.tensor_copy(rows_f[:, 0:2, :], rows_i[:, :, :]))
            nc.vector.tensor_reduce(span[:, 0:1], rows_f[:, 1, :], AX.X, ALU.min)
            step(nc.vector.tensor_reduce(span[:, 1:2], rows_f[:, 1, :], AX.X, ALU.max))
            step(nc.vector.tensor_scalar(span_b[:, :], span[:, :], float(P), None, ALU.is_ge))
            for b in range(2, NM):
                step(nc.vector.scalar_tensor_tensor(out=span_b[:, :], in0=span[:, :], scalar=float(b * P),
                                                    in1=span_b[:, :], op0=ALU.is_ge, op1=ALU.add))
            step(nc.vector.tensor_scalar(base[:, :], span_b[:, 0:1], float(P), None, ALU.mult))
            step(nc.vector.tensor_tensor(code[:, :], span_b[:, 1:2], span_b[:, 0:1], ALU.is_gt))
            nc.vector.scalar_tensor_tensor(out=code[:, :], in0=code[:, :], scalar=4.0, in1=span_b[:, 0:1], op0=ALU.mult, op1=ALU.add)
            nc.vector.tensor_scalar(rows_f[:, 2, :], rows_f[:, 1, :], base[:, 0:1], None, ALU.subtract).then_inc(s_idxT, 1)
            dve.wait_ge(s_idxT, 2)
            step(nc.vector.tensor_tensor(code_row[:, :, :], ps[0:1, 6, 0:ET].rearrange("p (g t) -> p g t", t=G), pow8[:, :, :], ALU.mult))
            step(nc.vector.tensor_reduce(pack_f[:, :], code_row[:, :, :], AX.X, ALU.add))
            nc.vector.tensor_copy(pack_i[:, :], pack_f[:, :])
            nc.vector.tensor_copy(node_f[:, :, :].rearrange("p t j -> p j t"),
                                  ps[:, 7, 0:3 * ET].rearrange("p (j t) -> p j t", j=3)).then_inc(s_spanok, 1)
            dve.wait_ge(s_spanok, 1)

            def count_onehots(q, s):
                dve.wait_ge(s_ohu, q + 1)
                c = bass.ds(q, 1)
                nc.vector.tensor_scalar(onehot[:, s, 0, :], iota_f[:, :], node_f[:, c, 0], None, ALU.is_equal)
                nc.vector.tensor_scalar(onehot[:, s, 1, :], iota_f[:, :], node_f[:, c, 2], None, ALU.is_equal).then_inc(s_oh, 1)

            dve.wait_ge(s_gconst, 5 + G)
            for a, b, t in ((0, T_HO, 0), (T_HO, T_HO + T_OO, 1), (T_HO + T_OO, ET, 2)):
                step(nc.vector.tensor_scalar(tabl_f[:, a:b, :], node_f[:, a:b, 0:2], float(t * N), None, ALU.add))
            nc.vector.tensor_copy(tabl_i[:, :, :], tabl_f[:, :, :]).then_inc(s_idxok, 1)

            roots = [0]

            def rsqrt(out, val):
                roots[0] += 1
                nc.vector.tensor_copy(rs_in[:, :], val).then_inc(s_rsin, 1)
                dve.wait_ge(s_rsin, roots[0])
                dve.wait_ge(s_root, roots[0])
                step(nc.vector.reciprocal(out, rs_root[:, :]))
                step(nc.vector.tensor_tensor(rs_t[:, :], out, out, ALU.mult))
                step(nc.vector.tensor_tensor(rs_t[:, :], rs_t[:, :], rs_in[:, :], ALU.mult))
                step(nc.vector.tensor_scalar(rs_t[:, :], rs_t[:, :], -0.5, 1.5, ALU.mult, ALU.add))
                return nc.vector.tensor_tensor(out, out, rs_t[:, :], ALU.mult)

            def row_stats(m, row):
                for i in range(2):
                    ins = nc.vector.bn_stats(stats[:, m, i, :], row[:, i * FB:(i + 1) * FB])
                step(ins)
                step(nc.vector.bn_aggr(mv[:, m, :], stats[:, m, :, :].rearrange("p a b -> p (a b)")))

            def row_scales():
                step(nc.vector.tensor_scalar(var_e[:, :], mv[:, :, 1], EPS, None, ALU.add))
                step(rsqrt(rstd[:, :], var_e[:, :]))

            def norm(m, src_row, dst_row):
                return nc.vector.tensor_scalar(dst_row, src_row, mv[:, m, 0:1], rstd[:, m:m + 1], ALU.subtract, ALU.mult)

            for m in range(NM):
                dve.wait_ge(s_x[m], 16)
                row_stats(m, gath[:, m, :])
            row_scales()
            for m in range(NM):
                norm(m, gath[:, m, :], hrow[:, m, :]).then_inc(s_norm, 1)

            def low(dst, high, b, count):
                dve.wait_ge(s_th, count)
                nc.vector.tensor_tensor(dst, ps[:, b, :], f32(high), ALU.subtract).then_inc(s_tl, 1)

            for k in range(KT):
                low(actT_l[:, k, :], actT_h[:, k, :], k, k + 1)

            def low_w(q, k):
                dve.wait_ge(s_high, q * KT + k + 1)
                nc.vector.tensor_tensor(ring_l[:, k, :], raw[:, k % RAW, :], f32(ring_h[:, k, :]), ALU.subtract).then_inc(s_low, 1)

            def copy_b(q):
                for m in range(NM):
                    bank_done(dve, q, m)
                    dve.wait_ge(s_st[m], q * 16)
                    nc.vector.tensor_tensor(stage[:, m, :], ps[:, NM + m, :], bias3[:, q // 4, q % NN * FB:(q % NN + 1) * FB],
                                            ALU.add).then_inc(s_copied, 1)

            def edge(q):
                s = q % GB
                dve.wait_ge(s_g[s], q // GB * 16 + 16)
                nc.vector.scalar_tensor_tensor(out=gath[:, s, :], in0=gath[:, s, :], scalar=0.0, in1=wa_b[:, :],
                                               op0=ALU.max, op1=ALU.mult, accum_out=lg[:, q:q + 1]).then_inc(s_edge, 1)

            def split_logits(a, b):
                dve.wait_ge(s_edge, GB + b)
                step(nc.vector.tensor_scalar(lgr[:, a:b], lg[:, a:b], ba[:, 0:1], None, ALU.add))
                for i in range(3):
                    step(nc.vector.tensor_copy(lgp[:, i, a:b], lgr[:, a:b]))
                    if i < 2:
                        step(nc.vector.tensor_tensor(lgr[:, a:b], lgr[:, a:b], lgp[:, i, a:b], ALU.subtract))
                step(nc.vector.tensor_copy(lgs[:, :, a:b], lgp[:, :, a:b]))

            def logit_onehots(q):
                dve.wait_ge(s_ohu, ET + q + 1)
                for j, e in ((0, 0), (1, 2)):
                    ins = nc.vector.tensor_scalar(onehot[:, q % OS, j, :], iota_f[:, :], node_f[:, q, e:e + 1], None, ALU.is_equal)
                ins.then_inc(s_oh, 1)

            def inverse_counts(t, k):
                dve.wait_ge(s_ccopy, t + 1)
                step(nc.vector.tensor_scalar(logit_d[:, t, k, :], count_d[:, t, k, :], 1.0, None, ALU.max))
                nc.vector.reciprocal(logit_d[:, t, k, :], logit_d[:, t, k, :])

            def copy_kind(t):
                dve.wait_ge(s_kind, t + 1)
                nc.vector.tensor_tensor(logit_d[:, t, :, :], ps[:, 0:NM, :], logit_d[:, t, :, :], ALU.mult).then_inc(s_kfree, 1)

            def mask_kind(t):
                dve.wait_ge(s_kfree, t + 1)
                step(nc.vector.tensor_scalar(mask[:, :, :], count_d[:, t, :, :], 0.0, -BIG, ALU.is_equal, ALU.mult))
                for k in range(NM):
                    ins = nc.vector.tensor_tensor_reduce(out=logit_d[:, t, k, :], in0=logit_d[:, t, k, :], in1=mask[:, k, :],
                                                         scale=1.0, scalar=-BIG, op0=ALU.add, op1=ALU.max,
                                                         accum_out=mx3[:, t, k:k + 1])
                step(ins)

            with dve.Fori(0, 3) as c:
                for k in range(KT):
                    low_w(c, k)
                    for j in range(2):
                        count_onehots(c * 2 * G + 2 * k + j, (2 * k + j) % OS)
            for k in range(KT):
                low_w(3, k)
                for j in range(2):
                    count_onehots(ET - 2 * G + 2 * k + j, (2 * k + j) % OS)
                if k == 0:
                    dve.wait_ge(s_bias, 48)
                    copy_b(2)
            dve.wait_ge(s_const, 32)

            INVERSE = {4: [(0, k) for k in range(NM)], 5: [(1, 0), (1, 1)], 6: [(1, 2), (1, 3)],
                       7: [(2, 0)], 8: [(2, 1)], 9: [(2, 2)], 10: [(2, 3)]}
            e = 0
            for q in range(4, CH_EDGE):
                inv = list(INVERSE.get(q, ()))
                if q > 4:
                    split_logits((q - 5) * G, (q - 4) * G)
                for k in range(KT):
                    low_w(q, k)
                    if 5 <= q and (q - 5) * G + k < T_HO:
                        logit_onehots((q - 5) * G + k)
                    if inv and (q == 4 or k in (3, 7)):
                        inverse_counts(*inv.pop(0))
                    if k == 2 and not is_a(q - 1):
                        copy_b(q - 1)
                    if (q, k) == (CH_EDGE - 1, 6):
                        copy_kind(0)
                    for _ in range(2 if q == 4 and k > 3 else 0 if q == 4 else 1):
                        if e < T_HO + T_OO:
                            edge(e)
                            e += 1
            q = CH_EDGE
            split_logits(7 * G, T_HO + T_OO)
            for k in range(KT):
                low_w(q, k)
                logit_onehots(T_HO + k)
                if k == 2:
                    copy_b(q - 1)
            for k in range(KT):
                low_w(q + 1, k)
                if k < 2:
                    logit_onehots(T_HO + 8 + k)
            for k in range(KT):
                low_w(q + 2, k)
                if k == 0:
                    copy_kind(1)
                if k == 3:
                    edge(62)
                    edge(63)
                    split_logits(62, ET)
                if k == 4:
                    logit_onehots(62)
                    logit_onehots(63)
            for k in range(KT):
                low_w(q + 3, k)
                if k == 3:
                    copy_kind(2)
            mask_kind(0)
            mask_kind(1)
            mask_kind(2)

            step(nc.vector.tensor_tensor(mx[:, :], mx3[:, 0, :], mx3[:, 1, :], ALU.max))
            step(nc.vector.tensor_tensor(mx[:, :], mx[:, :], mx3[:, 2, :], ALU.max))
            nc.vector.tensor_scalar(nmx[:, :], mx[:, :], -1.0, None, ALU.mult).then_inc(s_mx, 1)
            q = CH_EDGE + 4
            for i in range(4):
                dve.wait_ge(s_st[i], 16 * (CH_EDGE + 2))
            step(nc.vector.tensor_tensor(adj[:, :, :], count_d[:, 0, :, :], count_d[:, 1, :, :], ALU.add))
            step(nc.vector.tensor_tensor(adj[:, :, :], adj[:, :, :], count_d[:, 2, :, :], ALU.add))
            for k in range(NM):
                ins = nc.vector.scalar_tensor_tensor(out=adj[:, k, :], in0=iota_f[:, :], scalar=rowid[:, k:k + 1],
                                                     in1=adj[:, k, :], op0=ALU.is_equal, op1=ALU.add)
            ins.then_inc(s_adj, 1)
            for t in range(3):
                dve.wait_ge(s_exp, NM * (t + 1))
                ins = nc.vector.tensor_tensor(logit_d[:, t, :, :], logit_d[:, t, :, :], count_d[:, t, :, :], ALU.mult)
                if t:
                    step(ins)
                    step(nc.vector.tensor_tensor(logit_d[:, 0, :, :], logit_d[:, 0, :, :], logit_d[:, t, :, :], ALU.add))
            step(nc.vector.tensor_reduce(den[:, :], logit_d[:, 0, :, :], AX.X, ALU.add))
            step(nc.vector.tensor_scalar(den[:, :], den[:, :], 1e-30, None, ALU.max))
            step(nc.vector.reciprocal(rden[:, :], den[:, :]))
            for k in range(NM):
                ins = nc.vector.tensor_scalar(logit_d[:, 0, k, :], logit_d[:, 0, k, :], rden[:, k:k + 1], None, ALU.mult)
            ins.then_inc(s_att, 1)
            dve.wait_ge(s_hr_h, NM)
            for m in range(NM):
                nc.vector.tensor_tensor(hrow_l[:, m, :], hrow[:, m, :], f32(hrow_h[:, m, :]), ALU.subtract).then_inc(s_hr_l, 1)
            for k in range(NM):
                low(attT_l[:, k, :], attT_h[:, k, :], k, TP_H + k + 1)
            dve.wait_ge(s_deg, 1)
            rsqrt(dinv[:, :], ps[:, 4, 0:NM]).then_inc(s_dinv, 1)
            dve.wait_ge(s_adjs, 1)
            nc.vector.tensor_tensor(adj_l[:, :, :], adj[:, :, :], f32(adj_h[:, :, :]), ALU.subtract).then_inc(s_adjs, 1)
            for k in range(KT):
                if k == NM:
                    dve.wait_ge(s_deg, 2)
                    nc.vector.tensor_copy(wrow[:, :], ps[:, 5, 0:NM]).then_inc(s_dinv, 1)
                low(actT_l[:, k, :], actT_h[:, k, :], k, TP_ATT + k + 1)
            for m in range(NM):
                dve.wait_ge(s_topl[m], 16)
                dve.wait_ge(s_bias2, 48)
                nc.vector.tensor_tensor(topsum[:, m, :], topsum[:, m, :], bias3[:, 0 if m == 0 else 1, :], ALU.add).then_inc(s_top, 1)
            for c in range(4):
                for k in range(KT):
                    low_w(q + c, k)
            dve.wait_ge(s_top, NM)

            def low_w1(q, k, b):
                dve.wait_ge(s_high, q * KT + k + 1)
                nc.vector.tensor_tensor(ring_l[:, k, :], ps[:, b, :], f32(ring_h[:, k, :]), ALU.subtract).then_inc(s_low, 1)

            for i, (m, n) in enumerate(UPD):
                chunk_done(dve, q + UPD_CHUNK[i])
                c = slice(n * FB, (n + 1) * FB)
                nc.vector.tensor_tensor(topsum[:, m, c], topsum[:, m, c], ps[:, n * NM + m, :], ALU.add).then_inc(s_bsum, 1)
            q += 4
            for i, (m, n) in enumerate(UPD):
                dve.wait_ge(s_brelu, i + 1)
                dve.wait_ge(s_xr[m], 16)
                c = slice(n * FB, (n + 1) * FB)
                nc.vector.tensor_tensor(hrow[:, m, c], hrow[:, m, c], topsum[:, m, c], ALU.add).then_inc(s_x1, 1)
            for k in range(KT):
                low_w1(q, k, k)
            dve.wait_ge(s_x1, 8)
            dve.wait_ge(s_dinv, 2)
            for m in range(NM):
                row_stats(m, hrow[:, m, :])
            row_scales()
            for m in range(NM):
                step(norm(m, hrow[:, m, :], topsum[:, m, :]))
                nc.vector.tensor_scalar(topsum[:, m, :], topsum[:, m, :], 0.0, dinv[:, m:m + 1], ALU.max, ALU.mult).then_inc(s_norm, 1)
            for m in range(NM):
                dve.wait_ge(s_hr_h, NM + m + 1)
                nc.vector.tensor_tensor(hrow_l[:, m, :], topsum[:, m, :], f32(hrow_h[:, m, :]), ALU.subtract).then_inc(s_hr_l, 1)
            for k in range(KT):
                low(actT_l[:, k, :], actT_h[:, k, :], k, TP_Z + k + 1)
            for k in range(NM):
                low_w1(q + 1, k, NM + k)

            def outputs(n):
                c = slice(n * FB, (n + 1) * FB)
                chunk_done(dve, q + n)
                for m in range(NM):
                    step(nc.vector.scalar_tensor_tensor(out=topsum[:, m, c], in0=bias3[:, 2, c], scalar=wrow[:, m:m + 1],
                                                        in1=ps[:, m, :], op0=ALU.mult, op1=ALU.add))
                    nc.vector.scalar_tensor_tensor(out=topsum[:, m, c], in0=topsum[:, m, c], scalar=dinv[:, m:m + 1],
                                                   in1=hrow[:, m, c], op0=ALU.mult, op1=ALU.add).then_inc(s_out, 1)

            outputs(0)
            for k in range(NM, KT):
                low_w1(q + 1, k, k)
            outputs(1)


_INS = ['x', 'src', 'dst', 'L0_gnn_W_hh', 'L0_gnn_b_hh', 'L0_gnn_W_oo', 'L0_gnn_b_oo', 'L0_gnn_W_ho', 'L0_gnn_b_ho',
        'L0_gnn_W_a', 'L0_gnn_b_a', 'L0_gnn_W_hn', 'L0_gnn_b_hn', 'L0_gnn_W_on', 'L0_gnn_b_on', 'L1_gnn_W', 'L1_gnn_b']


def kernel(**inputs):
    import numpy as _np
    import concourse.bacc as _bacc
    from concourse import mybir as _mybir
    from concourse.bass_utils import run_bass_kernel_spmd as _run

    nc = _bacc.Bacc("TRN2", target_bir_lowering=False, num_devices=1)
    arrays, args = {}, []
    for name in _INS:
        a = _np.ascontiguousarray(inputs[name])
        arrays[f"in_{name}_dram"] = a
        args.append(nc.dram_tensor(f"in_{name}_dram", a.shape, _mybir.dt.from_np(a.dtype), kind="ExternalInput").ap())
    out = nc.dram_tensor("out_dram", inputs['x'].shape, _mybir.dt.float32, kind="ExternalOutput").ap()
    gnn_kernel(nc, *args, out)
    r = _run(nc, [arrays], core_ids=[0])
    return r.results[0]["out_dram"]
```

```python
from contextlib import ExitStack

import concourse.bass as bass
from concourse import mybir

P = 128
FB = 512
ALU = mybir.AluOpType
ACT = mybir.ActivationFunctionType
AX = mybir.AxisListType
F32 = mybir.dt.float32
F32R = mybir.dt.float32r
U16 = mybir.dt.uint16
BF16 = mybir.dt.bfloat16
FP16 = mybir.dt.float16
I32 = mybir.dt.int32
U32 = mybir.dt.uint32

E_HH, E_OO = 256, 1280
NH = 128
EPS = 1e-5
TINY = 1e-30
BIG = 1e30


def gnn_kernel(nc, x, src, dst, W_hh, b_hh, W_oo, b_oo, W_ho, b_ho, W_a, b_a,
               W_hn, b_hn, W_on, b_on, W1, b1, out):
    N, D = x.shape
    E = src.shape[0]
    NM = N // P
    KT = D // P
    NN = D // FB
    ET = E // P
    T_HH, T_OO = E_HH // P, E_OO // P
    T_HO = ET - T_HH - T_OO
    EARLY = T_HH + T_OO
    assert NM == 4 and KT == 8 and NN == 2 and N == FB and NH == P

    with ExitStack() as ctx:
        def sem(name):
            return ctx.enter_context(nc.semaphore(name))

        BASE = 16512
        assert BASE >= nc.sbuf_base
        at = {}

        def sb(name, shape, dt, size=None, over=None, shift=0):
            width = mybir.dt.size(dt)
            for n in shape[1:]:
                width *= n
            if over is None:
                off = at.get("end", BASE)
                at["end"] = off + -(-(size or width) // 32) * 32
            else:
                off = at[over] + shift
            at[name] = off
            return nc.alloc_sbuf_tensor_at(name, shape, dt, offset=off)

        actT_h = sb("actT_h", [P, KT, N], F32R)
        actT_l = sb("actT_l", [P, KT, N], F32R)
        hrow = sb("hrow", [P, NM, D], F32)
        ring_h = sb("ring_h", [P, KT, FB], F32R)
        ring_l = sb("ring_l", [P, KT, FB], F32R)
        RAW = 8
        raw = sb("raw", [P, RAW, FB], F32)
        GB = 8
        gath = sb("gath", [P, GB, D], F32)
        logit_d = sb("logit_d", [P, 3, NM, N], F32)
        count_d = sb("count_d", [P, 3, NM, N], U16)
        OS = 4
        G, TC = 8, 7
        topsum = sb("topsum", [P, NM, D], F32)
        onehot = sb("onehot", [P, OS, 4, N], BF16, over="topsum")
        stage = sb("stage", [P, 4, FB], F32)
        bias2 = sb("bias2", [P, 2, D], F32)
        wa_b = sb("wa_b", [P, D], F32)
        iota_f = sb("iota_f", [P, N], FP16)
        ident = sb("ident", [P, P], F32)
        ident_b = sb("ident_b", [P, P], BF16)
        zeros_r = sb("zeros_r", [P, N], BF16)
        rows_i = sb("rows_i", [ET, 2, P], I32, over="logit_d")
        rows_f = sb("rows_f", [ET, 3, P], F32, over="logit_d", shift=8 * P)
        span = sb("span", [ET, 2], F32)
        span_b = sb("span_b", [ET, 2], F32)
        base = sb("base", [ET, 1], F32)
        code = sb("code", [ET, 1], F32)
        GROUPS = {g: -(-ET // g) for g in (G, TC)}
        pow8 = sb("pow8", [1, G, G + 3], F32)
        code_row = sb("code_row", [1, ET + G], F32)
        code_w = sb("code_w", [1, ET + G], F32)
        pack_f = sb("pack_f", [1, G + 3], F32)
        pack_i = {g: sb(f"pack{g}_i", [1, GROUPS[g]], I32) for g in (G, TC)}
        node_f = sb("node_f", [P, ET, 3], F32)
        tabl_f = sb("tabl_f", [P, ET, 2], F32, over="logit_d", shift=20 * P)
        tabl_i = sb("tabl_i", [P, ET, 2], U32)
        tabl_s = sb("tabl_s", [P, GB, 2], U32)
        lg = sb("lg", [P, ET], F32)
        lgr = sb("lgr", [P, ET], F32)
        lgp = sb("lgp", [P, 3, ET], BF16)
        lgs = sb("lgs", [P, 3, ET], F32)
        ba = sb("ba", [P, 1], F32)
        stats = sb("stats", [P, NM, 2, 6], F32)
        mv = sb("mv", [P, NM, 2], F32)
        rstd = sb("rstd", [P, NM], F32)
        mx3 = sb("mx3", [P, 3, NM], F32)
        mx = sb("mx", [P, NM], F32)
        nmx = sb("nmx", [P, NM], F32)
        den3 = sb("den3", [P, NM, 3], F32)
        den = sb("den", [P, NM], F32)
        rden = sb("rden", [P, NM], F32)
        rowid = sb("rowid", [P, NM], F32)
        ones = sb("ones", [P, 1], F32)
        var_e = sb("var_e", [P, NM], F32)
        rs_in = sb("rs_in", [P, NM], F32)
        rs_root = sb("rs_root", [P, NM], F32)
        rs_t = sb("rs_t", [P, NM], F32)
        dinv = sb("dinv", [P, NM], F32)
        wrow = sb("wrow", [P, NM], F32)
        assert at["end"] <= nc.sbuf_usable_end

        hrow_h = sb("hrow_h", [P, NM, D], F32R, over="gath")
        hrow_l = sb("hrow_l", [P, NM, D], F32R, over="gath", shift=4 * NM * D)
        w1row = sb("w1row", [P, 4, D], F32, over="logit_d", shift=4 * NM * N)
        attT_h = sb("attT_h", [P, NM, N], F32R, over="logit_d", shift=4 * NM * N)
        attT_l = sb("attT_l", [P, NM, N], F32R, over="logit_d", shift=8 * NM * N)
        mask_b = [sb("mask_ho", [P, NM, N], BF16, over="logit_d", shift=4 * (2 * NM * N + 2 * N)),
                  sb("mask_oo", [P, NM, N], BF16, over="bias2", shift=4 * D),
                  sb("mask_hh", [P, NM, N], BF16, over="bias2")]
        adj = sb("adj", [P, NM, N], F32, over="stage")
        adj_h = sb("adj_h", [P, NM, N], F32R, over="logit_d")
        adj_l = sb("adj_l", [P, NM, N], F32R, over="count_d")

        ps = ctx.enter_context(nc.psum_tensor("ps", [P, 8, FB], F32))
        tab_a = nc.dram_tensor("tab_a", [3 * N, D], F32).ap()
        tab_b = nc.dram_tensor("tab_b", [3 * N, D], F32).ap()
        top_d = nc.dram_tensor("top_d", [N, D], F32).ap()

        s_x = [sem(f"x_loaded{m}") for m in range(NM)]
        s_idx = sem("edges_loaded")
        s_const = sem("consts_loaded")
        s_bias = sem("bias_loaded")
        s_w1row = sem("w1_loaded")
        s_raw = [sem(f"raw_loaded{i}") for i in range(RAW)]
        s_high = sem("w_high_ready")
        s_low = sem("w_low_ready")
        s_slot = sem("w_slots_free")
        s_bank = sem("table_banks_done")
        s_copied = sem("table_banks_free")
        s_st = [sem(f"stage_stored{i}") for i in range(4)]
        s_topl = [sem(f"top_loaded{m}") for m in range(NM)]
        s_mask = sem("masks_ready")
        s_part = sem("onehot_parts_ready")
        s_pool = sem("pool_chain")
        s_gconst = sem("consts_made")
        s_v = sem("vector_chain")
        s_rsin = sem("rsqrt_input")
        s_root = sem("square_roots")
        s_h = sem("h_rows")
        s_norm = sem("h_normed")
        s_tp = sem("transposed_banks")
        s_th = sem("transposed_high")
        s_tl = sem("transposed_low")
        s_idxT = sem("edges_transposed")
        s_spanok = sem("edge_blocks_ready")
        s_idxok = sem("edges_ready")
        s_ga = [sem(f"gathered_src{i}") for i in range(GB)]
        s_g = [sem(f"gathered{i}") for i in range(GB)]
        s_cdone = sem("counts_ready")
        s_ccopy = sem("counts_copied")
        s_edge = sem("gather_slots_free")
        s_stg = sem("index_staged")
        s_seen = sem("index_seen")
        s_oh = sem("onehots_ready")
        s_ohu = sem("onehot_slots_free")
        s_kind = sem("kind_counted")
        s_kfree = sem("kind_banks_free")
        s_mx = sem("row_max_ready")
        s_exp = sem("exp_done")
        s_rden = sem("row_sums_ready")
        s_att = sem("attention_ready")
        s_top = sem("top_banks_free")
        s_hr_h = sem("rows_high")
        s_hr_l = sem("rows_low")
        s_xr = [sem(f"residual_loaded{m}") for m in range(NM)]
        s_updbank = sem("last_update_banks")
        s_lastbank = sem("last_output_banks")
        s_bsum = sem("update_summed")
        s_adj = sem("adj_ready")
        s_adjs = sem("adj_split")
        s_deg = sem("deg_banks")
        s_dinv = sem("dinv_ready")
        s_out = sem("out_rows")
        s_outst = [sem(f"out_stored{i}") for i in range(2 * NM)]


        def passes(hi, lo, mh, ml):
            return ((hi, mh), (hi, ml), (lo, mh))

        block = ctx.enter_context(nc.Block())

        KINDS = ((W_ho, b_ho), (W_oo, b_oo), (W_hh, b_hh))
        CH_EDGE = 3 * 2 * NN
        hn, on = (W_hn, (0,)), (W_on, (1, 2, 3))
        NODE = [[(w, r, n, ms) for (w, ms), n in order]
                for r, order in ((0, ((on, 0), (hn, 0), (hn, 1), (on, 1))), (D, ((hn, 0), (hn, 1), (on, 0), (on, 1))))]
        TP_H = KT
        TP_ATT = TP_H + NM
        TP_Z = TP_ATT + KT
        TP_W1 = TP_Z + KT
        TP_G = TP_W1 + KT

        @block.sync
        def _(sp):
            for m in range(NM):
                sp.dma_start(gath[:, m, :], x[m * P:(m + 1) * P, :]).then_inc(s_x[m], 16)

            def load(w, row, n, q, k):
                sp.wait_ge(s_low, q * KT + k + 1)
                sp.dma_start(raw[:, k % RAW, :], w[bass.ds(row + k * P, P), n * FB:(n + 1) * FB]).then_inc(s_raw[k % RAW], 16)

            for t, (w, _) in enumerate(KINDS):
                with sp.Fori(0, 2) as half:
                    for n in range(NN):
                        for k in range(KT):
                            load(w, half * D, n, (half * NN + n) + t * 2 * NN, k)
            q = CH_EDGE
            for w, row, n, _ in NODE[0] + NODE[1]:
                for k in range(KT):
                    load(w, row, n, q, k)
                q += 1
            for n in range(NN):
                sp.wait_ge(s_tp, TP_Z if n == 0 else TP_W1)
                sp.dma_start(w1row[:, :, :], W1[n * FB:(n + 1) * FB, :].rearrange("(o p) i -> p o i", p=P)).then_inc(s_w1row, 16)
            for n in range(NN):
                for m in range(NM):
                    i = n * NM + m
                    sp.wait_ge(s_out, i + 1)
                    sp.dma_start(out[m * P:(m + 1) * P, n * FB:(n + 1) * FB], topsum[:, m, n * FB:(n + 1) * FB]).then_inc(s_outst[i], 16)
            for i in range(2 * NM):
                sp.wait_ge(s_outst[i], 16)

        @block.gpsimd
        def _(pool):
            nc.gpsimd.iota(iota_f[:, :], [[1, N]], base=0, channel_multiplier=0,
                           allow_small_or_imprecise_dtypes=True).then_inc(s_gconst, 1)
            nc.gpsimd.memset(zeros_r[:, :], 0.0).then_inc(s_gconst, 1)
            nc.gpsimd.memset(ident[:, :], 0.0).then_inc(s_pool, 1)
            pool.wait_ge(s_pool, 1)
            nc.gpsimd.affine_select(out=ident[:, :], in_=ident[:, :], compare_op=ALU.not_equal, fill=1.0,
                                    base=0, pattern=[[-1, P]], channel_multiplier=1).then_inc(s_gconst, 1)
            pool.wait_ge(s_gconst, 3)
            nc.gpsimd.tensor_copy(ident_b[:, :], ident[:, :]).then_inc(s_gconst, 1)
            nc.gpsimd.iota(rowid[:, :], [[P, NM]], base=0, channel_multiplier=1,
                           allow_small_or_imprecise_dtypes=True).then_inc(s_gconst, 1)
            for j in range(G):
                nc.gpsimd.memset(pow8[:, j, :], float(8 ** j)).then_inc(s_gconst, 1)
            nc.gpsimd.memset(code_row[:, :], 0.0).then_inc(s_gconst, 1)
            nc.gpsimd.memset(ones[:, :], 1.0).then_inc(s_gconst, 1)
            for m in range(NM):
                pool.wait_ge(s_x[m], 16)
            pool.dma_start(wa_b[:, :], W_a.rearrange("d a -> a d").partition_broadcast(P)).then_inc(s_const, 16)
            pool.dma_start(ba[:, :], b_a.rearrange("(a d) -> a d", a=1).partition_broadcast(P)).then_inc(s_const, 16)

            def bias(place, b):
                pool.dma_start(bias2[:, place, :], b.rearrange("(a d) -> a d", a=1).partition_broadcast(P)).then_inc(s_bias, 16)

            bias(0, b_ho)
            bias(1, b_oo)

            pool.wait_ge(s_idxok, 1)

            def gather_src(q, s, kinds):
                pool.wait_ge(s_edge, q + 1)
                nc.gpsimd.tensor_copy(tabl_s[:, s, :], tabl_i[:, bass.ds(q, 1), :].rearrange("p a b -> p (a b)")).then_inc(s_stg, 1)
                pool.wait_ge(s_stg, q + 1)
                pool.sem_inc(s_seen, 1)
                pool.indirect_dma_start(out=gath[:, s, :], out_offset=None, in_=tab_a[0:kinds * N, :],
                                        in_offset=bass.IndirectOffsetOnAxis(ap=tabl_s[:, s, 0:1], axis=0)).then_inc(s_ga[s], 16)

            def gather_dst(s, u, kinds):
                pool.wait_ge(s_ga[s], u * 16 + 16)
                pool.sem_inc(s_seen, 1)
                pool.indirect_dma_start(out=gath[:, s, :], out_offset=None, in_=tab_b[0:kinds * N, :],
                                        in_offset=bass.IndirectOffsetOnAxis(ap=tabl_s[:, s, 1:2], axis=0),
                                        compute_op=ALU.add).then_inc(s_g[s], 16)

            def tables_landed(kinds):
                for i in range(4):
                    pool.wait_ge(s_st[i], 64 * kinds)

            def gather_run(first, end, kinds, pending=0):
                for q in range(first, end):
                    gather_src(q, q % GB, kinds)
                    if q - LAG >= first - pending:
                        gather_dst((q - LAG) % GB, (q - LAG) // GB, kinds)

            def gather_rest(end, kinds):
                for q in range(end - LAG, end):
                    gather_dst(q % GB, q // GB, kinds)

            LAG = 3
            for i in range(4):
                pool.wait_ge(s_st[i], 32)
            for q in range(GB):
                gather_src(q, q, 1)
            tables_landed(1)
            pool.wait_ge(s_copied, NM + NM * 4)
            for q in range(GB - LAG):
                gather_dst(q, 0, 1)
            bias(0, b_hh)
            with pool.Fori(1, T_HO // GB) as i:
                for s in range(GB):
                    gather_src(i * GB + s, s, 1)
                    gather_dst((s - LAG) % GB, i if s >= LAG else i - 1, 1)
            gather_run(T_HO // GB * GB, T_HO, 1, LAG)
            gather_rest(T_HO, 1)
            tables_landed(2)
            gather_run(T_HO, T_HO + T_OO, 2)
            gather_rest(T_HO + T_OO, 2)
            tables_landed(3)
            for q in range(T_HO + T_OO, ET):
                gather_src(q, q % GB, 3)
            for q in range(T_HO + T_OO, ET):
                gather_dst(q % GB, q // GB, 3)
            pool.wait_ge(s_ohu, OS + 2 * ET)
            for i in range(4):
                pool.wait_ge(s_st[i], 16 * (CH_EDGE + 2))
            bias(0, b_hn)
            bias(1, b_on)
            for m in range(NM):
                pool.dma_start(topsum[:, m, :], top_d[m * P:(m + 1) * P, :]).then_inc(s_topl[m], 16)
            pool.wait_ge(s_hr_l, NM)
            for m in range(NM):
                pool.dma_start(hrow[:, m, :], x[m * P:(m + 1) * P, :]).then_inc(s_xr[m], 16)
            pool.wait_ge(s_top, NM)
            bias(0, b1)

        def chunk_done(eng, q):
            eng.wait_ge(s_slot, KT + q * KT + KT)

        def bank_done(eng, q, m):
            if m < NM - 1:
                eng.wait_ge(s_bank, q * (NM - 1) + m + 1)
            else:
                chunk_done(eng, q)

        FIRST_COUNTS = 2
        LAST_COUNTS = FIRST_COUNTS + ET // (2 * KT) - 1
        SUM_AT = {(6 + i, k): i * TC + k for i in range(6) for k in range(TC)}
        SUM_AT |= {(12, k): 42 + k for k in range(8)}
        SUM_AT |= {(13, k): 50 + k for k in range(2)}
        SUM_AT |= {(13, 4 + k): 52 + k for k in range(4)}
        SUM_AT |= {(14, k): 56 + k for k in range(6)}
        SUM_AT |= {(15, k): 62 + k for k in range(2)}
        assert sorted(SUM_AT.values()) == list(range(ET))
        EARLIER = 12
        EDGE_AT = {divmod(c * KT + k - EARLIER, KT): q for (c, k), q in SUM_AT.items() if q < ET - 2} | {(14, 0): ET - 2, (14, 1): ET - 1}
        ONEHOT_AT = {divmod(c * KT + k - 1, KT): q for (c, k), q in SUM_AT.items() if q < ET - 2} | {(14, 6): ET - 2, (14, 7): ET - 1}
        SPLIT_AT = {}
        for c in range(6, 16):
            tiles = [q for (c2, _), q in SUM_AT.items() if c2 == c]
            SPLIT_AT[(c - 1, KT - 1) if c < 15 else (14, 4)] = (min(tiles), max(tiles) + 1)
        SLOT, SLOT_FREE, user = {}, {}, {s: ET - OS + s for s in range(OS)}
        for (_, k), q in sorted(SUM_AT.items()):
            SLOT[q] = k % OS
            SLOT_FREE[q] = OS + user[k % OS] + 1
            user[k % OS] = ET + q
        LAST_OF_KIND = (T_HO - 1, T_HO + T_OO - 1, ET - 1)

        def is_a(q):
            return q // NN % 2 == 0

        @block.scalar
        def _(act):
            for j, e in enumerate((src, dst)):
                rows = e.rearrange("(t p) -> t p", p=P)
                to = 0
                for first, n in ((EARLY, T_HO), (T_HH, T_OO), (0, T_HH)):
                    act.dma_start(rows_i[to:to + n, j, :], rows[first:first + n, :]).then_inc(s_idx, 16)
                    to += n

            def root(i):
                act.wait_ge(s_rsin, i + 1)
                nc.scalar.activation(rs_root[:, :], rs_in[:, :], ACT.Sqrt).then_inc(s_root, 1)

            root(0)
            for m in range(NM):
                act.wait_ge(s_norm, m + 1)
                nc.scalar.activation(hrow[:, m, :], hrow[:, m, :], ACT.Relu).then_inc(s_h, 1)

            def high(dst, b, count):
                act.wait_ge(s_tp, count)
                nc.scalar.copy(dst, ps[:, b, :]).then_inc(s_th, 1)

            for k in range(KT):
                high(actT_h[:, k, :], k, k + 1)

            def round_w(q, k):
                act.wait_ge(s_raw[k % RAW], (q * (KT // RAW) + k // RAW) * 16 + 16)
                act.wait_ge(s_slot, q * KT + k + 1)
                nc.scalar.copy(ring_h[:, k, :], raw[:, k % RAW, :]).then_inc(s_high, 1)

            def counts(t):
                act.wait_ge(s_cdone, t + 1)
                nc.scalar.copy(count_d[:, t, :, :], ps[:, 0:NM, :]).then_inc(s_ccopy, 1)

            def table(q, m):
                n, r = q % NN, q // 4 * N + m * P
                return (tab_a if is_a(q) else tab_b)[r:r + P, n * FB:(n + 1) * FB]

            def copy_a(q):
                for m in range(NM):
                    bank_done(act, q, m)
                    if q:
                        act.wait_ge(s_st[m], q * 16)
                    nc.scalar.copy(stage[:, m, :], ps[:, NM + m, :]).then_inc(s_copied, 1)
                    act.wait_ge(s_copied, NM + q * NM + m + 1)
                    act.dma_start(table(q, m), stage[:, m, :]).then_inc(s_st[m], 16)

            def store_b(q):
                for m in range(NM):
                    act.wait_ge(s_copied, NM + q * NM + m + 1)
                    act.dma_start(table(q, m), stage[:, m, :]).then_inc(s_st[m], 16)

            top_at = [0]

            def copy_top(c):
                chunk_done(act, CH_EDGE + c)
                for m in NODE[0][c][3]:
                    i = top_at[0]
                    top_at[0] += 1
                    n = NODE[0][c][2]
                    act.wait_ge(s_st[i % 4], 16 * (CH_EDGE + i // 4))
                    nc.scalar.copy(stage[:, i % 4, :], ps[:, NM + m, :]).then_inc(s_copied, 1)
                    act.wait_ge(s_copied, NM + CH_EDGE * NM + i + 1)
                    act.dma_start(top_d[m * P:(m + 1) * P, n * FB:(n + 1) * FB], stage[:, i % 4, :]).then_inc(s_st[i % 4], 16)

            def logit_parts(q):
                act.wait_ge(s_oh, ET + q + 1)
                s = SLOT[q]
                for i in (1, 2, 0):
                    ins = nc.scalar.mul(onehot[:, s, 1 + i, :], onehot[:, s, 1, :], lgs[:, i, q:q + 1])
                ins.then_inc(s_part, 1)

            def rounds(p, end):
                for i in range(p, end):
                    round_w(i // KT, i % KT)

            AHEAD = 2

            def edge_chunk(q):
                for k in range(KT):
                    if q * KT + k + AHEAD < (CH_EDGE + 4) * KT:
                        rounds(q * KT + k + AHEAD, q * KT + k + AHEAD + 1)
                    if (q, k) in SUM_AT:
                        logit_parts(SUM_AT[q, k])
                    if k == 2 and q:
                        if q > CH_EDGE:
                            copy_top(q - 1 - CH_EDGE)
                        elif is_a(q - 1):
                            copy_a(q - 1)
                    if k == 4 and 0 < q <= CH_EDGE and not is_a(q - 1):
                        store_b(q - 1)
                    if (q, k) == (LAST_COUNTS, 3):
                        counts(0)
                    if (q, k) == (LAST_COUNTS, 7):
                        counts(1)
                        counts(2)

            rounds(0, AHEAD)
            for q in range(CH_EDGE + 4):
                edge_chunk(q)
            q = CH_EDGE + 4
            act.wait_ge(s_edge, ET + GB)
            for m in range(NM):
                nc.scalar.copy(hrow_h[:, m, :], hrow[:, m, :]).then_inc(s_hr_h, 1)
            act.wait_ge(s_mx, 1)
            for k in range(NM):
                for t in range(3):
                    nc.scalar.activation(logit_d[:, t, k, :], logit_d[:, t, k, :], ACT.Exp,
                                         bias=nmx[:, k:k + 1]).then_inc(s_exp, 1)
            for k in range(NM):
                act.wait_ge(s_rden, k + 1)
                nc.scalar.mul(logit_d[:, 0, k, :], logit_d[:, 0, k, :], rden[:, k:k + 1]).then_inc(s_att, 1)
                if k == 0:
                    copy_top(3)
            for k in range(NM):
                high(attT_h[:, k, :], k, TP_H + k + 1)
            for k in range(KT):
                if k == 3:
                    root(1)
                if k < 4:
                    round_w(q, k)
                high(actT_h[:, k, :], k, TP_ATT + k + 1)
            rounds(q * KT + 4, (q + 1) * KT)
            act.wait_ge(s_adj, 1)
            nc.scalar.copy(adj_h[:, :, :], adj[:, :, :]).then_inc(s_adjs, 1)
            rounds((q + 1) * KT, (q + 4) * KT)
            q += 4

            def high_w1(q, k, b, count):
                act.wait_ge(s_tp, count)
                act.wait_ge(s_slot, q * KT + k + 1)
                nc.scalar.copy(ring_h[:, k, :], ps[:, b, :]).then_inc(s_high, 1)

            for k in range(NM):
                high_w1(q, k, k, TP_Z + k + 1)
            root(2)
            for m in range(NM):
                act.wait_ge(s_norm, NM + m + 1)
                nc.scalar.activation(hrow_h[:, m, :], topsum[:, m, :], ACT.Relu).then_inc(s_hr_h, 1)
            for k in range(NM, KT):
                high_w1(q, k, k, TP_Z + k + 1)
            for k in range(KT):
                high(actT_h[:, k, :], k, TP_W1 + k + 1)
            for k in range(KT):
                high_w1(q + 1, k, NM + k % NM, TP_G + k + 1)

        @block.tensor
        def _(pe):
            pe.sem_inc(s_slot, KT)
            pe.sem_inc(s_ohu, OS)
            pe.wait_ge(s_gconst, 7 + G)

            def codes(g, size):
                return nc.values_load_multi_w_load_instructions(
                    pack_i[size][0:1, bass.ds(g, 1)], engines=[mybir.EngineType.PE], min_val=0, max_val=8 ** size - 1,
                    skip_runtime_bounds_check_because="the codes are packed on the chip, 3 bits each")[1][0]

            def accumulate(code, t, s, parts):
                lo = code >> (3 * t)

                def block(j):
                    for i in range(parts):
                        mm = nc.tensor.matmul(ps[:, bass.ds((lo + j) & 3, 1), :].rearrange("p a n -> p (a n)"),
                                              onehot[:, s, 1 + i, j * P:(j + 1) * P], onehot[:, s, 0, :],
                                              start=False, stop=False, skip_group_check=True)
                    return mm

                with pe.If((lo & 4) > 0):
                    for j in range(1, NM):
                        block(j)
                block(0).then_inc(s_ohu, 1)

            def open_banks():
                for b in range(NM):
                    nc.tensor.matmul(ps[:, b, :], zeros_r[:, 0:P], zeros_r[:, :], start=True, stop=False, skip_group_check=True)

            def open_masked(t):
                pe.wait_ge(s_mask, t + 1)
                for b in range(NM):
                    nc.tensor.matmul(ps[:, b, :], ident_b[:, :], mask_b[t][:, b, :], start=True, stop=False, skip_group_check=True)

            def close_banks(done):
                for b in range(NM):
                    mm = nc.tensor.matmul(ps[:, b, :], zeros_r[:, 0:P], zeros_r[:, :], start=False, stop=True, skip_group_check=True)
                mm.then_inc(done, 1)

            pe.wait_ge(s_h, NM)
            for k in range(KT):
                for m in range(NM):
                    mm = nc.tensor.transpose(ps[:, k, m * P:(m + 1) * P], hrow[:, m, k * P:(k + 1) * P], ident[:, :])
                mm.then_inc(s_tp, 1)
            pe.wait_ge(s_tl, TP_H)

            def product(b, pairs):
                for i, (w, v) in enumerate(pairs):
                    mm = nc.tensor.matmul(ps[:, b, :], w, v, start=(i == 0), stop=(i == len(pairs) - 1))
                return mm

            def chunk(q, first, ms, bank_free=None, before=None, after=None, counted=False):
                for k in range(KT):
                    if before:
                        before(k)
                    pe.wait_ge(s_low, RAW + q * KT + k + 1)
                    for m in ms:
                        if k == 0 and bank_free:
                            bank_free(m)
                        for i, (w, v) in enumerate(passes(actT_h[:, k, m * P:(m + 1) * P], actT_l[:, k, m * P:(m + 1) * P],
                                                          ring_h[:, k, :], ring_l[:, k, :])):
                            mm = nc.tensor.matmul(ps[:, first + m, :], w, v, start=(k == 0 and i == 0),
                                                  stop=(k == KT - 1 and i == 2))
                        if counted and k == KT - 1 and m < NM - 1:
                            mm.then_inc(s_bank, 1)
                    mm.then_inc(s_slot, 1)
                    if after:
                        after(k)

            def edge_chunk(q, before=None, after=None):
                chunk(q, NM, range(NM), lambda m: pe.wait_ge(s_copied, q * NM + m + 1), before, after, counted=True)

            reg = [None]

            def count_tiles(g0, k):
                if k % 4 == 0:
                    reg[0] = codes(g0 + k // 4, G)
                for j in range(2):
                    t = 2 * k + j
                    pe.wait_ge(s_oh, g0 * G + t + 1)
                    accumulate(reg[0], t % G, t % OS, 1)

            def last_counts(k):
                for j in range(2):
                    t = 2 * k + j
                    q = ET - 2 * G + t
                    if q == T_HO or q == T_HO + T_OO:
                        kind = 1 if q == T_HO else 2
                        pe.wait_ge(s_ccopy, kind)
                        open_banks()
                    if t % G == 0:
                        reg[0] = codes(q // G, G)
                    pe.wait_ge(s_oh, q + 1)
                    accumulate(reg[0], t % G, t % OS, 1)
                    if q + 1 in (T_HO, T_HO + T_OO, ET):
                        close_banks(s_cdone)

            def add_logits(q, place, s):
                pe.wait_ge(s_part, q + 1)
                accumulate(reg[0], place, s, 3)

            def uniform_sums(i, k):
                if k == 0:
                    reg[0] = codes(i, TC)
                if k < TC:
                    add_logits(i * TC + k, k, k % OS)

            def last_sums(c, k):
                q = SUM_AT.get((c, k))
                if q is None:
                    return
                if q in (T_HO, T_HO + T_OO):
                    t = 1 if q == T_HO else 2
                    pe.wait_ge(s_kfree, NM * t)
                    open_masked(t)
                if q % TC == 0 or (c, k) == (12, 0) or q in (T_HO, T_HO + T_OO):
                    reg[0] = codes(q // TC, TC)
                add_logits(q, q % TC, SLOT[q])
                if q in LAST_OF_KIND:
                    close_banks(s_kind)


            edge_chunk(0)
            pe.wait_ge(s_idxT, 1)
            for j in range(3):
                nc.tensor.transpose(ps[:, 0, j * ET:(j + 1) * ET], rows_f[:, j, :], ident[0:ET, 0:ET])
            nc.tensor.transpose(ps[0:1, 1, 0:ET], code[:, :], ident[0:ET, 0:ET]).then_inc(s_idxT, 1)
            edge_chunk(1)
            pe.wait_ge(s_spanok, 1)
            open_banks()
            with pe.Fori(0, 3) as c:
                edge_chunk(c + FIRST_COUNTS, after=lambda k: count_tiles(c * 2, k))
            edge_chunk(LAST_COUNTS, after=last_counts)
            pe.wait_ge(s_ccopy, 3)
            open_masked(0)
            with pe.Fori(0, 6) as i:
                edge_chunk(i + 6, before=lambda k: uniform_sums(i, k))
            q = CH_EDGE
            base = NM + NM * CH_EDGE
            waits = (NM * CH_EDGE + 1, None, base + 4, None)
            for c, (_, _, _, ms) in enumerate(NODE[0]):
                free = None
                if waits[c]:
                    free = lambda m: pe.wait_ge(s_copied, waits[c] + (m if c == 0 else 0))
                chunk(q + c, NM, ms, free, before=lambda k: last_sums(q + c, k))
            pe.wait_ge(s_kfree, 3 * NM)
            q += 4
            for m in range(NM):
                pe.wait_ge(s_att, m + 1)
                for k in range(NM):
                    mm = nc.tensor.transpose(ps[:, k, m * P:(m + 1) * P], logit_d[:, 0, m, k * P:(k + 1) * P], ident[:, :])
                    if m == NM - 1:
                        mm.then_inc(s_tp, 1)
            pe.wait_ge(s_tl, TP_ATT)
            pe.wait_ge(s_hr_l, NM)
            for f in range(KT):
                if f == 1:
                    pe.wait_ge(s_copied, base + 8)
                if f == 3:
                    pe.wait_ge(s_adj, 1)
                    for m in range(NM):
                        for k in range(NM):
                            mm = nc.tensor.matmul(ps[:, 6, m:m + 1], adj[:, k, m * P:(m + 1) * P], ones[:, :], start=(k == 0), stop=(k == NM - 1))
                    mm.then_inc(s_deg, 1)
                if f == 6:
                    pe.wait_ge(s_dinv, 1)
                    for m in range(NM):
                        for k in range(NM):
                            mm = nc.tensor.matmul(ps[:, 7, m:m + 1], adj[:, k, m * P:(m + 1) * P], dinv[:, k:k + 1], start=(k == 0), stop=(k == NM - 1))
                    mm.then_inc(s_deg, 1)
                if f == 7:
                    pe.wait_ge(s_dinv, 2)
                c = slice(f * P, (f + 1) * P)
                product(f, [p for k in range(NM) for p in passes(hrow_h[:, k, c], hrow_l[:, k, c], attT_h[:, k, :], attT_l[:, k, :])]
                        ).then_inc(s_tp, 1)
            pe.wait_ge(s_tl, TP_Z)

            def w1_transposed(k, b):
                for o in range(4):
                    mm = nc.tensor.transpose(ps[:, b, o * P:(o + 1) * P], w1row[:, o, k * P:(k + 1) * P], ident[:, :])
                mm.then_inc(s_tp, 1)

            for c, (_, _, n, ms) in enumerate(NODE[1][:3]):
                chunk(q + c, n * NM, ms)
            q += 3
            for m in NODE[1][3][3]:
                for k in range(KT):
                    pe.wait_ge(s_low, RAW + q * KT + k + 1)
                    for i, (w, v) in enumerate(passes(actT_h[:, k, m * P:(m + 1) * P], actT_l[:, k, m * P:(m + 1) * P],
                                                      ring_h[:, k, :], ring_l[:, k, :])):
                        mm = nc.tensor.matmul(ps[:, NM + m, :], w, v, start=(k == 0 and i == 0), stop=(k == KT - 1 and i == 2))
                    if m == NM - 1:
                        mm.then_inc(s_slot, 1)
                    elif k == KT - 1:
                        mm.then_inc(s_updbank, 1)
                if m == NM - 2:
                    pe.wait_ge(s_w1row, 16)
                    pe.wait_ge(s_bsum, 5)
                    for k in range(NM):
                        w1_transposed(k, k)
            q += 1
            pe.wait_ge(s_bsum, 8)
            for k in range(NM, KT):
                w1_transposed(k, k)
            pe.wait_ge(s_adjs, 2)
            for k in range(NM):
                pe.wait_ge(s_hr_l, NM + k + 1)
                pe.wait_ge(s_low, RAW + q * KT + NM)
                for f in range(NM):
                    c = slice(f * P, (f + 1) * P)
                    for i, (w, v) in enumerate(passes(hrow_h[:, k, c], hrow_l[:, k, c], adj_h[:, k, :], adj_l[:, k, :])):
                        mm = nc.tensor.matmul(ps[:, f, :], w, v, start=(k == 0 and i == 0), stop=(k == NM - 1 and i == 2))
                    if k == NM - 1:
                        mm.then_inc(s_tp, 1)
            for f in range(NM, KT):
                c = slice(f * P, (f + 1) * P)
                pe.wait_ge(s_low, RAW + q * KT + f + 1)
                product(f, [p for k in range(NM) for p in passes(hrow_h[:, k, c], hrow_l[:, k, c], adj_h[:, k, :], adj_l[:, k, :])]
                        ).then_inc(s_tp, 1)
            pe.wait_ge(s_w1row, 32)
            for k in range(NM):
                pe.wait_ge(s_tl, TP_Z + NM + k + 1)
                w1_transposed(k, NM + k)
            pe.wait_ge(s_tl, TP_Z + KT)
            chunk(q, 0, range(NM))
            for k in range(NM, KT):
                pe.wait_ge(s_low, RAW + (q + 1) * KT + k - NM + 1)
                w1_transposed(k, k)
            for m in range(NM):
                pe.wait_ge(s_out, m + 1)
                for k in range(KT):
                    pe.wait_ge(s_low, RAW + (q + 1) * KT + k + 1)
                    for i, (w, v) in enumerate(passes(actT_h[:, k, m * P:(m + 1) * P], actT_l[:, k, m * P:(m + 1) * P],
                                                      ring_h[:, k, :], ring_l[:, k, :])):
                        mm = nc.tensor.matmul(ps[:, m, :], w, v, start=(k == 0 and i == 0), stop=(k == KT - 1 and i == 2))
                mm.then_inc(s_lastbank, 1)

        @block.vector
        def _(dve):
            dve.sem_inc(s_low, RAW)
            dve.sem_inc(s_copied, NM)
            dve.sem_inc(s_edge, GB)
            chain = [0]

            def step(ins):
                chain[0] += 1
                ins.then_inc(s_v, 1)
                dve.wait_ge(s_v, chain[0])

            f32 = lambda ap: ap.bitcast(F32)

            def count_onehots(q, s):
                dve.wait_ge(s_ohu, q + 1)
                nc.vector.tensor_scalar(onehot[:, s, 0, :], iota_f[:, :], node_f[:, q, 0:1], None, ALU.is_equal)
                nc.vector.tensor_scalar(onehot[:, s, 1, :], iota_f[:, :], node_f[:, q, 2:3], None, ALU.is_equal).then_inc(s_oh, 1)

            roots = [0]

            def rsqrt(out, val):
                roots[0] += 1
                nc.vector.tensor_copy(rs_in[:, :], val).then_inc(s_rsin, 1)
                dve.wait_ge(s_rsin, roots[0])
                dve.wait_ge(s_root, roots[0])
                step(nc.vector.reciprocal(out, rs_root[:, :]))
                step(nc.vector.tensor_tensor(rs_t[:, :], out, out, ALU.mult))
                step(nc.vector.tensor_tensor(rs_t[:, :], rs_t[:, :], rs_in[:, :], ALU.mult))
                step(nc.vector.tensor_scalar(rs_t[:, :], rs_t[:, :], -0.5, 1.5, ALU.mult, ALU.add))
                return nc.vector.tensor_tensor(out, out, rs_t[:, :], ALU.mult)

            def row_stats(m, row):
                for i in range(2):
                    ins = nc.vector.bn_stats(stats[:, m, i, :], row[:, i * FB:(i + 1) * FB])
                step(ins)
                step(nc.vector.bn_aggr(mv[:, m, :], stats[:, m, :, :].rearrange("p a b -> p (a b)")))

            def row_scales():
                step(nc.vector.tensor_scalar(var_e[:, :], mv[:, :, 1], EPS, None, ALU.add))
                step(rsqrt(rstd[:, :], var_e[:, :]))

            def norm(m, src_row, dst_row):
                return nc.vector.tensor_scalar(dst_row, src_row, mv[:, m, 0:1], rstd[:, m:m + 1], ALU.subtract, ALU.mult)

            for m in range(NM):
                dve.wait_ge(s_x[m], 16)
                row_stats(m, gath[:, m, :])
            row_scales()
            for m in range(NM):
                norm(m, gath[:, m, :], hrow[:, m, :]).then_inc(s_norm, 1)

            def low(dst, high, b, count):
                dve.wait_ge(s_th, count)
                nc.vector.tensor_tensor(dst, ps[:, b, :], f32(high), ALU.subtract).then_inc(s_tl, 1)

            for k in range(KT):
                low(actT_l[:, k, :], actT_h[:, k, :], k, k + 1)

            def low_w(q, k):
                dve.wait_ge(s_high, q * KT + k + 1)
                nc.vector.tensor_tensor(ring_l[:, k, :], raw[:, k % RAW, :], f32(ring_h[:, k, :]), ALU.subtract).then_inc(s_low, 1)

            def copy_b(q):
                dve.wait_ge(s_bias, 32 if q < 8 else 48)
                for m in range(NM):
                    bank_done(dve, q, m)
                    dve.wait_ge(s_st[m], q * 16)
                    nc.vector.tensor_tensor(stage[:, m, :], ps[:, NM + m, :], bias2[:, q // 4 % 2, q % NN * FB:(q % NN + 1) * FB],
                                            ALU.add).then_inc(s_copied, 1)

            def edge(q):
                s = q % GB
                dve.wait_ge(s_g[s], q // GB * 16 + 16)
                nc.vector.scalar_tensor_tensor(out=gath[:, s, :], in0=gath[:, s, :], scalar=0.0, in1=wa_b[:, :],
                                               op0=ALU.max, op1=ALU.mult, accum_out=lg[:, q:q + 1]).then_inc(s_edge, 1)

            def split_logits(a, b):
                dve.wait_ge(s_edge, GB + b)
                step(nc.vector.tensor_scalar(lgr[:, a:b], lg[:, a:b], ba[:, 0:1], None, ALU.add))
                for i in range(3):
                    step(nc.vector.tensor_copy(lgp[:, i, a:b], lgr[:, a:b]))
                    if i < 2:
                        step(nc.vector.tensor_tensor(lgr[:, a:b], lgr[:, a:b], lgp[:, i, a:b], ALU.subtract))
                step(nc.vector.tensor_copy(lgs[:, :, a:b], lgp[:, :, a:b]))

            def logit_onehots(q):
                dve.wait_ge(s_ohu, SLOT_FREE[q])
                for j, e in ((0, 0), (1, 2)):
                    ins = nc.vector.tensor_scalar(onehot[:, SLOT[q], j, :], iota_f[:, :], node_f[:, q, e:e + 1], None, ALU.is_equal)
                ins.then_inc(s_oh, 1)

            def inverse_counts(t, k):
                dve.wait_ge(s_ccopy, t + 1)
                step(nc.vector.tensor_scalar(logit_d[:, t, k, :], count_d[:, t, k, :], 1.0, None, ALU.max))
                nc.vector.reciprocal(logit_d[:, t, k, :], logit_d[:, t, k, :])

            def make_mask(t):
                dve.wait_ge(s_ccopy, t + 1)
                nc.vector.tensor_scalar(mask_b[t][:, :, :], count_d[:, t, :, :], 0.0, -BIG, ALU.is_equal, ALU.mult).then_inc(s_mask, 1)

            def copy_kind(t):
                dve.wait_ge(s_kind, t + 1)
                for k in range(NM):
                    nc.vector.tensor_tensor_reduce(out=logit_d[:, t, k, :], in0=ps[:, k, :], in1=logit_d[:, t, k, :],
                                                   scale=1.0, scalar=-BIG, op0=ALU.mult, op1=ALU.max,
                                                   accum_out=mx3[:, t, k:k + 1]).then_inc(s_kfree, 1)

            for k in range(KT // 2):
                low_w(0, k)
            dve.wait_ge(s_idx, 96)
            dve.wait_ge(s_gconst, 7 + G)
            step(nc.vector.tensor_copy(rows_f[:, 0:2, :], rows_i[:, :, :]))
            nc.vector.tensor_reduce(span[:, 0:1], rows_f[:, 1, :], AX.X, ALU.min)
            step(nc.vector.tensor_reduce(span[:, 1:2], rows_f[:, 1, :], AX.X, ALU.max))
            step(nc.vector.tensor_scalar(span_b[:, :], span[:, :], float(P), None, ALU.is_ge))
            for b in range(2, NM):
                step(nc.vector.scalar_tensor_tensor(out=span_b[:, :], in0=span[:, :], scalar=float(b * P),
                                                    in1=span_b[:, :], op0=ALU.is_ge, op1=ALU.add))
            step(nc.vector.tensor_scalar(base[:, :], span_b[:, 0:1], float(P), None, ALU.mult))
            step(nc.vector.tensor_tensor(code[:, :], span_b[:, 1:2], span_b[:, 0:1], ALU.is_gt))
            nc.vector.scalar_tensor_tensor(out=code[:, :], in0=code[:, :], scalar=4.0, in1=span_b[:, 0:1], op0=ALU.mult, op1=ALU.add)
            nc.vector.tensor_scalar(rows_f[:, 2, :], rows_f[:, 1, :], base[:, 0:1], None, ALU.subtract).then_inc(s_idxT, 1)
            for k in range(KT // 2, KT):
                low_w(0, k)
            for k in range(KT // 2):
                low_w(1, k)
            dve.wait_ge(s_idxT, 2)
            step(nc.vector.tensor_copy(code_row[:, 0:ET], ps[0:1, 1, 0:ET]))
            for g, n in GROUPS.items():
                step(nc.vector.tensor_tensor(code_w[:, 0:g * n].rearrange("p (n t) -> p n t", t=g),
                                             code_row[:, 0:g * n].rearrange("p (n t) -> p n t", t=g),
                                             pow8[:, 0:g, 0:n].rearrange("p t n -> p n t"), ALU.mult))
                step(nc.vector.tensor_reduce(pack_f[:, 0:n], code_w[:, 0:g * n].rearrange("p (n t) -> p n t", t=g), AX.X, ALU.add))
                step(nc.vector.tensor_copy(pack_i[g][:, :], pack_f[:, 0:n]))
            nc.vector.tensor_copy(node_f[:, :, :].rearrange("p t j -> p j t"),
                                  ps[:, 0, 0:3 * ET].rearrange("p (j t) -> p j t", j=3)).then_inc(s_spanok, 1)
            dve.wait_ge(s_spanok, 1)
            for a, b, t in ((0, T_HO, 0), (T_HO, T_HO + T_OO, 1), (T_HO + T_OO, ET, 2)):
                step(nc.vector.tensor_scalar(tabl_f[:, a:b, :], node_f[:, a:b, 0:2], float(t * N), None, ALU.add))
            nc.vector.tensor_copy(tabl_i[:, :, :], tabl_f[:, :, :]).then_inc(s_idxok, 1)
            for k in range(KT // 2, KT):
                low_w(1, k)

            MASK_AT = {(LAST_COUNTS, 6): 0, (9, 5): 1, (12, 5): 2}
            INVERSE_AT = dict(zip([(c, k) for c in range(6, 12) for k in (3, 7)],
                                  [(t, k) for t in range(3) for k in range(NM)]))
            dve.wait_ge(s_const, 32)
            low_w(2, 0)
            for q in range(2, CH_EDGE + 4):
                for k in range(KT):
                    q1, k1 = divmod(q * KT + k + 1, KT)
                    if q1 < CH_EDGE + 4:
                        low_w(q1, k1)
                    if k == (0 if q <= LAST_COUNTS else 2) and q <= CH_EDGE and not is_a(q - 1):
                        copy_b(q - 1)
                    if q <= LAST_COUNTS:
                        for t in (2 * k, 2 * k + 1):
                            count_onehots((q - FIRST_COUNTS) * 2 * KT + t, t % OS)
                    if (q, k) in INVERSE_AT:
                        inverse_counts(*INVERSE_AT[q, k])
                    if (q, k) in MASK_AT:
                        make_mask(MASK_AT[q, k])
                    if (q, k) in ((13, 2), (15, 2)):
                        copy_kind(q - 13)
                    if (q, k) in EDGE_AT:
                        edge(EDGE_AT[q, k])
                    if (q, k) in SPLIT_AT:
                        split_logits(*SPLIT_AT[q, k])
                    if (q, k) in ONEHOT_AT:
                        logit_onehots(ONEHOT_AT[q, k])
                    if (q, k) == (14, 7):
                        copy_kind(1)

            dve.wait_ge(s_kfree, 3 * NM)
            step(nc.vector.tensor_tensor(mx[:, :], mx3[:, 0, :], mx3[:, 1, :], ALU.max))
            step(nc.vector.tensor_tensor(mx[:, :], mx[:, :], mx3[:, 2, :], ALU.max))
            nc.vector.tensor_scalar(nmx[:, :], mx[:, :], -1.0, None, ALU.mult).then_inc(s_mx, 1)
            q = CH_EDGE + 4

            def rows_low(m):
                dve.wait_ge(s_hr_h, m + 1)
                nc.vector.tensor_tensor(hrow_l[:, m, :], hrow[:, m, :], f32(hrow_h[:, m, :]), ALU.subtract).then_inc(s_hr_l, 1)

            rows_low(0)
            rows_low(1)
            for k in range(NM):
                for t in range(3):
                    dve.wait_ge(s_exp, 3 * k + t + 1)
                    ins = nc.vector.tensor_tensor_reduce(out=logit_d[:, t, k, :], in0=logit_d[:, t, k, :], in1=count_d[:, t, k, :],
                                                         scale=1.0, scalar=TINY if t == 0 else 0.0, op0=ALU.mult, op1=ALU.add,
                                                         accum_out=den3[:, k, t:t + 1])
                step(ins)
                nc.vector.tensor_tensor(logit_d[:, 0, k, :], logit_d[:, 0, k, :], logit_d[:, 1, k, :], ALU.add)
                step(nc.vector.tensor_reduce(den[:, k:k + 1], den3[:, k, :], AX.X, ALU.add))
                nc.vector.reciprocal(rden[:, k:k + 1], den[:, k:k + 1])
                nc.vector.tensor_tensor(logit_d[:, 0, k, :], logit_d[:, 0, k, :], logit_d[:, 2, k, :], ALU.add).then_inc(s_rden, 1)
            rows_low(2)
            rows_low(3)
            for k in range(NM):
                low(attT_l[:, k, :], attT_h[:, k, :], k, TP_H + k + 1)
            for i in range(4):
                dve.wait_ge(s_st[i], 16 * (CH_EDGE + 2))
            step(nc.vector.tensor_tensor(adj[:, :, :], count_d[:, 0, :, :], count_d[:, 1, :, :], ALU.add))
            step(nc.vector.tensor_tensor(adj[:, :, :], adj[:, :, :], count_d[:, 2, :, :], ALU.add))
            for k in range(NM):
                ins = nc.vector.scalar_tensor_tensor(out=adj[:, k, :], in0=iota_f[:, :], scalar=rowid[:, k:k + 1],
                                                     in1=adj[:, k, :], op0=ALU.is_equal, op1=ALU.add)
            ins.then_inc(s_adj, 1)
            for k in range(KT):
                if k == 3:
                    dve.wait_ge(s_deg, 1)
                    rsqrt(dinv[:, :], ps[:, 6, 0:NM]).then_inc(s_dinv, 1)
                if k == 6:
                    dve.wait_ge(s_deg, 2)
                    nc.vector.tensor_copy(wrow[:, :], ps[:, 7, 0:NM]).then_inc(s_dinv, 1)
                low(actT_l[:, k, :], actT_h[:, k, :], k, TP_ATT + k + 1)
                if k < 4:
                    low_w(q, k)
            for k in range(4, KT):
                low_w(q, k)
            def low_w1(q, k, b):
                dve.wait_ge(s_high, q * KT + k + 1)
                nc.vector.tensor_tensor(ring_l[:, k, :], ps[:, b, :], f32(ring_h[:, k, :]), ALU.subtract).then_inc(s_low, 1)

            def update(c):
                _, _, n, ms = NODE[1][c]
                h = slice(n * FB, (n + 1) * FB)
                for j, m in enumerate(ms):
                    if c == 3 and m < NM - 1:
                        dve.wait_ge(s_updbank, j + 1)
                    else:
                        if c == 3:
                            for k in range(NM):
                                low_w1(q + 4, k, k)
                        chunk_done(dve, q + c)
                    nc.vector.tensor_tensor(topsum[:, m, h], topsum[:, m, h], ps[:, n * NM + m, :], ALU.add).then_inc(s_bsum, 1)
                    bsums[0] += 1
                    dve.wait_ge(s_bsum, bsums[0])
                    dve.wait_ge(s_xr[m], 16)
                    step(nc.vector.scalar_tensor_tensor(out=hrow[:, m, h], in0=topsum[:, m, h], scalar=0.0, in1=hrow[:, m, h],
                                                        op0=ALU.max, op1=ALU.add))
                    nc.vector.bn_stats(stats[:, m, n, :], hrow[:, m, h])

            bsums = [0]
            for k in range(KT):
                low_w(q + 1, k)
            for k in range(KT):
                low_w(q + 2, k)
                if k == 2:
                    dve.wait_ge(s_adjs, 1)
                    nc.vector.tensor_tensor(adj_l[:, :, :], adj[:, :, :], f32(adj_h[:, :, :]), ALU.subtract).then_inc(s_adjs, 1)
                if k == 4:
                    for m in range(NM):
                        dve.wait_ge(s_topl[m], 16)
                        dve.wait_ge(s_bias, 16 * 5)
                        nc.vector.tensor_tensor(topsum[:, m, :], topsum[:, m, :], bias2[:, 0 if m == 0 else 1, :], ALU.add).then_inc(s_top, 1)
                    dve.wait_ge(s_top, NM)
            update(0)
            update(1)
            for k in range(KT):
                low_w(q + 3, k)
            update(2)
            update(3)

            q += 4
            for m in range(NM):
                step(nc.vector.bn_aggr(mv[:, m, :], stats[:, m, :, :].rearrange("p a b -> p (a b)")))
            row_scales()
            step(nc.vector.tensor_tensor(rstd[:, :], rstd[:, :], dinv[:, :], ALU.mult))

            def norm_h2(m):
                norm(m, hrow[:, m, :], topsum[:, m, :]).then_inc(s_norm, 1)

            norm_h2(0)
            for m in range(NM):
                if m < NM - 1:
                    norm_h2(m + 1)
                dve.wait_ge(s_hr_h, NM + m + 1)
                nc.vector.scalar_tensor_tensor(out=hrow_l[:, m, :], in0=topsum[:, m, :], scalar=0.0, in1=f32(hrow_h[:, m, :]),
                                               op0=ALU.max, op1=ALU.subtract).then_inc(s_hr_l, 1)
            for k in range(NM, KT):
                low_w1(q, k, k)
            for k in range(KT):
                low(actT_l[:, k, :], actT_h[:, k, :], k, TP_Z + k + 1)
            for k in range(NM):
                low_w1(q + 1, k, NM + k)

            dve.wait_ge(s_bias, 16 * 6)

            def outputs(n):
                c = slice(n * FB, (n + 1) * FB)
                if n == 0:
                    chunk_done(dve, q)
                for m in range(NM):
                    if n:
                        dve.wait_ge(s_lastbank, m + 1)
                    step(nc.vector.scalar_tensor_tensor(out=topsum[:, m, c], in0=bias2[:, 0, c], scalar=wrow[:, m:m + 1],
                                                        in1=ps[:, m, :], op0=ALU.mult, op1=ALU.add))
                    nc.vector.scalar_tensor_tensor(out=topsum[:, m, c], in0=topsum[:, m, c], scalar=dinv[:, m:m + 1],
                                                   in1=hrow[:, m, c], op0=ALU.mult, op1=ALU.add).then_inc(s_out, 1)

            outputs(0)
            for k in range(NM, KT):
                low_w1(q + 1, k, k)
            outputs(1)


_INS = ['x', 'src', 'dst', 'L0_gnn_W_hh', 'L0_gnn_b_hh', 'L0_gnn_W_oo', 'L0_gnn_b_oo', 'L0_gnn_W_ho', 'L0_gnn_b_ho',
        'L0_gnn_W_a', 'L0_gnn_b_a', 'L0_gnn_W_hn', 'L0_gnn_b_hn', 'L0_gnn_W_on', 'L0_gnn_b_on', 'L1_gnn_W', 'L1_gnn_b']


def kernel(**inputs):
    import numpy as _np
    import concourse.bacc as _bacc
    from concourse import mybir as _mybir
    from concourse.bass_utils import run_bass_kernel_spmd as _run

    nc = _bacc.Bacc("TRN2", target_bir_lowering=False, num_devices=1)
    arrays, args = {}, []
    for name in _INS:
        a = _np.ascontiguousarray(inputs[name])
        arrays[f"in_{name}_dram"] = a
        args.append(nc.dram_tensor(f"in_{name}_dram", a.shape, _mybir.dt.from_np(a.dtype), kind="ExternalInput").ap())
    out = nc.dram_tensor("out_dram", inputs['x'].shape, _mybir.dt.float32, kind="ExternalOutput").ap()
    gnn_kernel(nc, *args, out)
    r = _run(nc, [arrays], core_ids=[0])
    return r.results[0]["out_dram"]
```
